# Optimizing a Trainium2 kernel written in Bass

```python
import numpy as np
import jax
import jax.numpy as jnp

def _softmax(x, axis=-1):
    return jax.nn.softmax(x, axis=axis)
def _gelu(x):
    return jax.nn.gelu(x, approximate=True)
def _silu(x):
    return jax.nn.silu(x)
def _sigmoid(x):
    return jax.nn.sigmoid(x)
def _layernorm(x, axis=-1, eps=1e-5):
    m = jnp.mean(x, axis=axis, keepdims=True)
    v = jnp.var(x, axis=axis, keepdims=True)
    return (x - m) / jnp.sqrt(v + eps)
def _scatter_add(tgt, idx, src, axis=0):
    return tgt.at[idx].add(src)
def _segment_sum(src, seg, n):
    return jax.ops.segment_sum(src, seg, n)

kernel_name = 'mk_adj_preln_d2_adj_256_f80b5d'

def setup_inputs(seed: int = 0):
    np.random.seed(seed)
    _w = jnp.asarray
    def _rec_inputs():
        import jax
        import jax.numpy as jnp
        _gk = jax.random.key(seed)
        x = -0.0005146 + 1 * jax.random.normal(jax.random.fold_in(_gk, 1), (8, 2048, 256), jnp.float32)
        _a = jax.random.bernoulli(jax.random.fold_in(_gk, 2), 0.0078125, (8, 2048, 2048))
        adj = _a.astype(jnp.int32)
        return x, adj
    x, adj = _rec_inputs()
    def _L0_gnn_setup():
        import jax, jax.numpy as jnp
        import numpy as np
        B, N, C, OUT, S = (4, 2048, 256, 256, 25)
        DENSITY = 0.008
        key = jax.random.key(seed)
        kA, kX, kW = jax.random.split(key, 3)
        A = jax.random.bernoulli(kA, DENSITY, (B, N, N)).astype(jnp.int32)
        X = jax.random.normal(kX, (B, N, C), dtype=jnp.float32)
        W = jax.random.normal(kW, (2 * C, OUT), dtype=jnp.float32) * np.float32(1.0 / np.sqrt(2 * C))
        b = jnp.zeros((OUT,), dtype=jnp.float32)
        return {'A': A, 'X': X, 'W': W, 'b': b}
    _L0_gnn_all = _L0_gnn_setup()
    _L0_gnn_in = {k: v for k, v in _L0_gnn_all.items() if k in ('W', 'b', )}
    del _L0_gnn_all

    def _L1_gnn_setup():
        import jax, jax.numpy as jnp
        import numpy as np
        B, N, D = (8, 1024, 256)
        H, HO = (4, 64)
        T = 5
        NEG = -1000000000.0
        EPS = 1e-06
        key = jax.random.key(seed)
        ks = jax.random.split(key, 6)
        nodes_embed = jax.random.normal(ks[0], (B, N, D), dtype=jnp.float32)
        node_adj = jax.random.randint(ks[1], (B, N, N), 0, T + 1)
        W = jax.random.normal(ks[2], (H, D, HO), dtype=jnp.float32) * (1.0 / np.sqrt(D))
        a_src = jax.random.normal(ks[3], (H, T, HO), dtype=jnp.float32) * 0.1
        a_dst = jax.random.normal(ks[4], (H, T, HO), dtype=jnp.float32) * 0.1
        bias = jnp.zeros((H, HO), dtype=jnp.float32)
        ln_gamma = jnp.ones((H, HO), dtype=jnp.float32)
        ln_beta = jnp.zeros((H, HO), dtype=jnp.float32)
        return {'nodes_embed': nodes_embed, 'node_adj': node_adj, 'W': W, 'a_src': a_src, 'a_dst': a_dst, 'bias': bias, 'ln_gamma': ln_gamma, 'ln_beta': ln_beta}
    _L1_gnn_all = _L1_gnn_setup()
    _L1_gnn_in = {k: v for k, v in _L1_gnn_all.items() if k in ('W', 'a_src', 'a_dst', 'bias', 'ln_gamma', 'ln_beta', )}
    del _L1_gnn_all

    return {
        "x": x,
        "adj": adj,
        "L0_gnn_W": _L0_gnn_in["W"],
        "L0_gnn_b": _L0_gnn_in["b"],
        "L1_gnn_W": _L1_gnn_in["W"],
        "L1_gnn_a_src": _L1_gnn_in["a_src"],
        "L1_gnn_a_dst": _L1_gnn_in["a_dst"],
        "L1_gnn_bias": _L1_gnn_in["bias"],
        "L1_gnn_ln_gamma": _L1_gnn_in["ln_gamma"],
        "L1_gnn_ln_beta": _L1_gnn_in["ln_beta"],
    }

def reference(x, adj, L0_gnn_W, L0_gnn_b, L1_gnn_W, L1_gnn_a_src, L1_gnn_a_dst, L1_gnn_bias, L1_gnn_ln_gamma, L1_gnn_ln_beta):
    import jax
    import jax.numpy as jnp
    def _L0_gnn_ref(A, X, W, b):
        import jax, jax.numpy as jnp
        import numpy as np
        B, N, C, OUT, S = (4, 2048, 256, 256, 25)
        DENSITY = 0.008
        mask = A != 0
        neg_inf = jnp.float32(-jnp.inf)
        pri = -jnp.arange(N, dtype=jnp.float32)
        scores = jnp.where(mask, pri, neg_inf)
        vals, idx = jax.lax.top_k(scores, S)
        valid = vals > neg_inf
        feats = jax.vmap(lambda x, i: x[i])(X, idx)
        feats = jnp.where(valid[..., None], feats, neg_inf)
        agg = feats.max(axis=2)
        degree = mask.sum(axis=-1)
        agg = jnp.where((degree <= S)[..., None], jnp.maximum(agg, 0.0), agg)
        h = jnp.concatenate([X, agg], axis=-1)
        out = jax.nn.relu(jnp.einsum('bnf,fo->bno', h, W) + b)
        return out

    def _L1_gnn_ref(nodes_embed, node_adj, W, a_src, a_dst, bias, ln_gamma, ln_beta):
        import jax, jax.numpy as jnp
        import numpy as np
        B, N, D = (8, 1024, 256)
        H, HO = (4, 64)
        T = 5
        NEG = -1000000000.0
        EPS = 1e-06
        h = jnp.einsum('bnd,hde->bhne', nodes_embed, W)
        e_src = jnp.einsum('bhne,hte->bhtn', h, a_src)
        e_dst = jnp.einsum('bhne,hte->bhtn', h, a_dst)
        n_types = a_src.shape[1]
        weight = jnp.zeros(h.shape[:2] + (h.shape[2], h.shape[2]), dtype=h.dtype)
        for t in range(n_types):
            mask = (node_adj == t + 1).astype(h.dtype)[:, None]
            weight = weight + mask * (e_src[:, :, t, :, None] + e_dst[:, :, t, None, :])
        weight = jax.nn.leaky_relu(weight, negative_slope=0.01)
        weight = jnp.where(node_adj[:, None] == 0, NEG, weight)
        attention = jax.nn.softmax(weight, axis=-1)
        dst = jnp.einsum('bhij,bhje->bhie', attention, h) + bias[None, :, None, :]
        out = jax.nn.relu(dst) + h
        mu = out.mean(axis=-1, keepdims=True)
        var = out.var(axis=-1, keepdims=True)
        out = (out - mu) / jnp.sqrt(var + EPS) * ln_gamma[None, :, None, :] + ln_beta[None, :, None, :]
        b, hh, n, e = out.shape
        return out.transpose(0, 2, 1, 3).reshape(b, n, hh * e)

    h = jnp.maximum(_layernorm(x, axis=-1), 0.0)
    x = x + _L0_gnn_ref(adj, h, L0_gnn_W, L0_gnn_b)
    h = jnp.maximum(_layernorm(x, axis=-1), 0.0)
    x = x + _L1_gnn_ref(h, adj, L1_gnn_W, L1_gnn_a_src, L1_gnn_a_dst, L1_gnn_bias, L1_gnn_ln_gamma, L1_gnn_ln_beta)
    return x


_drawn_inputs = setup_inputs


def setup_inputs(seed=0):
    import zlib

    import numpy as np

    out = dict(_drawn_inputs(seed))
    spreads = {'L0_gnn_b': (0.0, 0.1),
     'L1_gnn_bias': (0.0, 0.1),
     'L1_gnn_ln_gamma': (1.0, 0.2),
     'L1_gnn_ln_beta': (0.0, 0.1)}
    factors = {'L1_gnn_a_src': 5.538, 'L1_gnn_a_dst': 2.91}
    for name, (base, spread) in spreads.items():
        noise = np.random.default_rng([zlib.crc32(name.encode()), seed]).standard_normal(out[name].shape)
        drawn = base * np.exp(spread * noise) if base else spread * noise
        out[name] = jnp.asarray(drawn.astype(out[name].dtype))
    for name, factor in factors.items():
        out[name] = (out[name] * factor).astype(out[name].dtype)
    return out
```

```python
from contextlib import ExitStack

import numpy as np

import concourse.bass as bass
from concourse import mybir

ALU = mybir.AluOpType
ACT = mybir.ActivationFunctionType
AX_X = mybir.AxisListType.X
F32 = mybir.dt.float32
BF16 = mybir.dt.bfloat16
I32 = mybir.dt.int32
U32 = mybir.dt.uint32

P = 128
B, N, C = 8, 2048, 256
S = 25
H, E = 4, 64
T = 5
NT = N // P
EPS0 = 1e-5
EPS1 = 1e-6
NEG = -1.0e9
SLOPE = 0.01
ROWS = N + 1
GB = 8
NG = N // GB
GPT = P // GB
RG = 5
NR = S // RG
V = 2 * E + 2
K3 = 3
Q = 4
NQ = NT // Q


class Chain:

    def __init__(self, eng, sem):
        self.eng, self.sem, self.n = eng, sem, 0

    def link(self, ins):
        self.n += 1
        ins.then_inc(self.sem, 1)
        self.eng.wait_ge(self.sem, self.n)


def free(eng, sem, n):
    if n > 0:
        eng.wait_ge(sem, n)


def over(ap, axis, shape):
    return ap.unsqueeze(axis).to_broadcast(shape)


def graph_layers(nc, x, adj, w0, b0, w1, a_src, a_dst, bias1, gamma1, beta1, c_ident, c_bits, c_base, c_bit, c_ofs, out):
    with ExitStack() as ctx:
        def sb(name, shape, dt=F32):
            return ctx.enter_context(nc.sbuf_tensor(name, shape, dt))

        def ps(name, shape, dt=F32):
            return ctx.enter_context(nc.psum_tensor(name, shape, dt))

        sems = []

        def sem(name):
            sems.append(ctx.enter_context(nc.semaphore(name)))
            return sems[-1]

        def reset():
            ids = sorted(s.num for s in sems)
            assert ids == list(range(ids[0], ids[-1] + 1))
            nc.gpsimd.dma_reset(range(ids[0], ids[-1] + 1))
            nc.gpsimd.sem_clear(range(ids[0], ids[-1] + 1))
            nc.all_engine_barrier()

        def scratch(name, shape, dt=F32):
            return nc.dram_tensor(name, shape, dt, kind="Internal").ap()

        table = scratch("table", (B * ROWS, C))
        maskT_d = scratch("maskT_d", (B, NT, P, NT, P), BF16)
        x1_d = scratch("x1_d", (B, NT, P, C))
        hp_d = scratch("hp_d", (B, NT, P, C))
        src_d = scratch("src_d", (B, H, N))
        table_g = table.rearrange("(b r) c -> b r c", b=B)

        ident = sb("ident", [P, P])
        identb = sb("identb", [P, P], BF16)
        bits_w = sb("bits_w", [P, GPT], BF16)
        base = sb("base", [P, NG])
        bitc = sb("bitc", [P, S, GB], I32)
        ofsc = sb("ofsc", [P, S, GB], I32)
        ones = sb("ones", [P, P])
        w0_sb = sb("w0_sb", [P, 4, C])
        b0_sb = sb("b0_sb", [1, C])
        r1 = sb("r1", [P, 2, C + 2 * H])
        bias_b = sb("bias_b", [P, H, E])
        gamma_b = sb("gamma_b", [P, H, E])
        beta_b = sb("beta_b", [P, H, E])
        zero_b = sb("zero_b", [B, C])
        mhalf = sb("mhalf", [P, 1])
        epsc = sb("epsc", [P, 2])

        x0 = [sb(f"x0_{i}", [P, Q, C]) for i in range(2)]
        st0 = sb("st0", [P, Q, 6])
        mv0 = sb("mv0", [P, Q, 2])
        rs0 = [sb(f"rs0_{i}", [P, Q]) for i in range(2)]
        nm0 = [sb(f"nm0_{i}", [P, Q]) for i in range(2)]

        adj_h = [sb(f"adj_h{i}", [P, N // 2], I32) for i in range(2)]
        mask_h = [sb(f"mask_h{i}", [P, N // 2], BF16) for i in range(2)]
        sq = sb("sq", [P, N // 2], BF16)
        chk = sb("chk", [P, 2 * NT])
        mT = [sb(f"mT{i}", [P, NT, P], BF16) for i in range(2)]
        key = sb("key", [P, NG])
        k32 = sb("k32", [P, 32])
        ki = sb("ki", [P, S], I32)
        b8 = sb("b8", [P, S], I32)
        an = sb("an", [P, S, GB], I32)
        sco = sb("sco", [P, S, GB])
        cand = sb("cand", [P, S * GB])
        c32 = sb("c32", [P, 32])
        rowbase = sb("rowbase", [P, 1])
        idx = [sb(f"idx{i}", [P, S], U32) for i in range(2)]
        gath = [sb(f"gath{g}", [P, RG, C]) for g in range(NR)]
        part = sb("part", [P, NR, C])
        hx = [sb(f"hx{i}", [P, 2, C]) for i in range(4)]
        agg = sb("agg", [P, C])
        hT = sb("hT", [P, 4, P])
        x1 = [sb(f"x1_{i}", [P, C]) for i in range(2)]
        st1 = sb("st1", [P, 6])
        mv1 = sb("mv1", [P, 2])
        rs1 = sb("rs1", [P, 2])
        h1 = sb("h1", [P, C])
        h1T = sb("h1T", [P, 2, P])
        hps = [sb(f"hps{i}", [P, C]) for i in range(2)]
        sd = sb("sd", [P, NT, 2 * H])
        eT = [sb(f"eT{i}", [H, P]) for i in range(2)]

        sd2 = sb("sd2", [P, NT, 2 * H])
        dmm = sb("dmm", [P, 2 * H])
        drow = sb("drow", [2 * H, 1])
        ddiag = sb("ddiag", [2 * H, 2 * H])
        dmax = sb("dmax", [P, 2 * H])
        tmpz = sb("tmpz", [P, NT, H])
        tmpn = sb("tmpn", [P, NT, H])
        tmpp = sb("tmpp", [P, NT, H])
        negd = sb("negd", [P, NT, H])
        eB = sb("eB", [P, NT, H])
        eB1 = sb("eB1", [P, NT, H])
        eA = sb("eA", [P, NT, H])
        eA1 = sb("eA1", [P, NT, H])
        hpl = [sb(f"hpl{i}", [P, 2, C]) for i in range(2)]
        vf = sb("vf", [P, 2 * H, V])
        flat = vf[:].rearrange("p a v -> p (a v)")
        asrc, adst, wa_tmp = (flat[:, i * C:(i + 1) * C].rearrange("p (h e) -> p h e", h=H) for i in range(3))
        val = sb("val", [P, NT * H, K3, V], BF16)
        maskq = [sb(f"maskq{i}", [P, Q, NT, P], BF16) for i in range(2)]
        srcb = [sb(f"srcb{i}", [P, Q * P]) for i in range(2)]
        gt = [sb(f"gt{i}", [P, Q * P], BF16) for i in range(4)]
        hq = sb("hq", [P, Q, C])
        gs = sb("gs", [P, Q, V])
        ms = sb("ms", [P, Q, E + 1])
        f0 = sb("f0", [P, Q, E + 1])
        f1 = sb("f1", [P, Q, E])
        rden = sb("rden", [P, Q])
        mean = sb("mean", [P, Q])
        var = sb("var", [P, Q])
        outq = x0

        acc = [ps(f"acc{i}", [P, 512]) for i in range(Q)]
        macc = ps("macc", [P, 512])
        tps = ps("tps", [P, 1024], BF16)
        kps = ps("kps", [P, 512])
        cps = ps("cps", [P, 512])

        const_in, const_ok = sem("const_in"), sem("const_ok")
        r1_ps, r1_ok = sem("r1_ps"), sem("r1_ok")
        dve_c, act_c = sem("dve_c"), sem("act_c")
        x0_in = [sem(f"x0_in{i}") for i in range(2)]
        x0_var, x0_root, x0_norm, x0_relu = sem("x0_var"), sem("x0_root"), sem("x0_norm"), sem("x0_relu")
        var1_ok, root1_ok, var2_ok, root2_ok = sem("var1_ok"), sem("root1_ok"), sem("var2_ok"), sem("root2_ok")
        x0_out = [sem(f"x0_out{i}") for i in range(2)]
        zero_out = sem("zero_out")
        adj_in = [sem(f"adj_in{i}") for i in range(2)]
        hx_in = [sem(f"hx_in{i}") for i in range(4)]
        mask_ok, chk_ok = sem("mask_ok"), sem("chk_ok")
        turn_ok, mT_ok, keys_ok, keys_used, idx_ok = sem("turn_ok"), sem("mT_ok"), sem("keys_ok"), sem("keys_used"), sem("idx_ok")
        g_in = [sem(f"g_in{s}") for s in range(S)]
        red_ok, agg_ok = sem("red_ok"), sem("agg_ok")
        hT_ps, hT_ok, lin_ok, x1_ok, ln1_ok, h1_ok = (sem("hT_ps"), sem("hT_ok"), sem("lin_ok"), sem("x1_ok"),
                                                      sem("ln1_ok"), sem("h1_ok"))
        h1T_ps, h1T_ok, hp_ps, hp_ok = sem("h1T_ps"), sem("h1T_ok"), sem("hp_ps"), sem("hp_ok")
        mT_out = [sem(f"mT_out{i}") for i in range(2)]
        x1_out = [sem(f"x1_out{i}") for i in range(2)]
        hp_out = [sem(f"hp_out{i}") for i in range(2)]
        e_out = [sem(f"e_out{i}") for i in range(2)]
        sd_ok = sem("sd_ok")
        dT_ps, dd_ok, db_ps, exp_in, exp_ok = sem("dT_ps"), sem("dd_ok"), sem("db_ps"), sem("exp_in"), sem("exp_ok")
        hpl_in = [sem(f"hpl_in{i}") for i in range(2)]
        hpl_used, hi_in, hi_ok, mid_ok, val_ok = (sem("hpl_used"), sem("hi_in"), sem("hi_ok"), sem("mid_ok"), sem("val_ok"))
        maskq_in = [sem(f"maskq_in{i}") for i in range(2)]
        srcb_in = [sem(f"srcb_in{i}") for i in range(2)]
        xh_in = sem("xh_in")
        gt_ok, gt_used = sem("gt_ok"), sem("gt_used")
        acc_used, macc_ok, macc_used = sem("acc_used"), sem("macc_ok"), sem("macc_used")
        unit_done = sem("unit_done")
        out_st = [sem(f"out_st{i}") for i in range(2)]

        W1N = C + 2 * H
        STEPS = NT + 2

        with nc.Block() as block:
            @block.sync
            def _(sp):
                def row_bc(a, n):
                    return a.rearrange("h e -> (h e)").partition_broadcast(n)

                for dst, src in ((ident[:], c_ident), (base[:], c_base), (bitc[:], c_bit), (ofsc[:], c_ofs),
                                 (bits_w[:], c_bits), (w0_sb[:], w0.rearrange("(k p) o -> p k o", p=P)),
                                 (b0_sb[:], b0.unsqueeze(0)),
                                 (bias_b[:].rearrange("p h e -> p (h e)"), row_bc(bias1, P)),
                                 (gamma_b[:].rearrange("p h e -> p (h e)"), row_bc(gamma1, P)),
                                 (beta_b[:].rearrange("p h e -> p (h e)"), row_bc(beta1, P)),
                                 (asrc, a_src[:, 0, :].partition_broadcast(P)),
                                 (adst, a_dst[:, 0, :].partition_broadcast(P))):
                    sp.dma_start(dst, src).then_inc(const_in, 16)
                for k in range(2):
                    sp.dma_start(r1[:, k, 0:C].rearrange("p (h e) -> p h e", h=H),
                                 w1[:, k * P:(k + 1) * P, :].rearrange("h p e -> p h e")).then_inc(const_in, 16)
                sp.wait_ge(const_ok, 2)
                sp.dma_start(table_g[:, N, :], zero_b[:]).then_inc(zero_out, 16)


                sp.wait_ge(zero_out, 16)

            @block.vector
            def _(dve):
                v = nc.vector
                link = Chain(dve, dve_c).link
                v.memset(ones[:], 1.0).then_inc(const_ok, 1)
                link(v.memset(rowbase[:], float(N)))
                v.memset(zero_b[:], 0.0).then_inc(const_ok, 1)
                v.memset(mhalf[:], -0.5)
                v.memset(epsc[:, 0:1], EPS0)
                v.memset(epsc[:, 1:2], EPS1).then_inc(const_ok, 1)
                dve.wait_ge(const_in, 16 * 14)
                v.tensor_copy(identb[:], ident[:]).then_inc(const_ok, 1)
                for k in range(2):
                    w = r1[:, k, 0:C].rearrange("p (h e) -> p h e", h=H)
                    for j, a in enumerate((asrc, adst)):
                        link(v.tensor_tensor(wa_tmp, w, a, ALU.mult))
                        link(v.tensor_reduce(r1[:, k, C + H * j:C + H * j + H], wa_tmp, AX_X, ALU.add))
                dve.sem_inc(r1_ok, 1)


        reset()

        with nc.Fori(0, B) as b:
            with nc.Block() as block:
                @block.sync
                def _(sp):
                    for q in range(NQ):
                        free(sp, x0_out[q % 2], q // 2 * 16)
                        sp.dma_start(x0[q % 2][:], x[b, q * Q * P:(q + 1) * Q * P, :].rearrange("(t p) c -> p t c", p=P))\
                          .then_inc(x0_in[q % 2], 16)

                @block.vector
                def _(dve):
                    v = nc.vector
                    link = Chain(dve, dve_c).link
                    for q in range(NQ):
                        dve.wait_ge(x0_in[q % 2], (q // 2 + 1) * 16)
                        for t in range(Q):
                            ins = v.bn_stats(st0[:, t, :], x0[q % 2][:, t, :])
                        link(ins)
                        for t in range(Q):
                            ins = v.bn_aggr(mv0[:, t, :], st0[:, t, :])
                        link(ins)
                        ins = v.tensor_copy(rs0[q % 2][:], mv0[:, :, 1])
                        ins.then_inc(x0_var, 1)
                        dve.wait_ge(x0_root, q + 1)
                        link(v.reciprocal(rs0[q % 2][:], rs0[q % 2][:]))
                        v.scalar_tensor_tensor(nm0[q % 2][:], mv0[:, :, 0], -1.0, rs0[q % 2][:], ALU.mult, ALU.mult)\
                         .then_inc(x0_norm, 1)

                @block.scalar
                def _(act):
                    for q in range(NQ):
                        act.wait_ge(x0_var, q + 1)
                        nc.scalar.activation(rs0[q % 2][:], rs0[q % 2][:], ACT.Sqrt, bias=epsc[:, 0:1]).then_inc(x0_root, 1)
                        act.wait_ge(x0_norm, q + 1)
                        for t in range(Q):
                            nc.scalar.activation(x0[q % 2][:, t, :], x0[q % 2][:, t, :], ACT.Relu,
                                                 bias=nm0[q % 2][:, t:t + 1], scale=rs0[q % 2][:, t:t + 1])\
                              .then_inc(x0_relu, 1)
                        act.wait_ge(x0_relu, (q + 1) * Q)
                        act.dma_start(table_g[b, q * Q * P:(q + 1) * Q * P, :].rearrange("(t p) c -> p t c", p=P),
                                      x0[q % 2][:]).then_inc(x0_out[q % 2], 16)
                    for i in range(2):
                        act.wait_ge(x0_out[i], NQ // 2 * 16)
            reset()

        def wait_hx(eng, b, k):
            eng.wait_ge(hx_in[k % 4], (k // 4 + 1) * 32)

        def turn_of_engines(b1, b2):
            both = b1 is not None and b2 is not None
            steps = range(STEPS) if b1 is not None else range(1, NT + 1)
            block = turns.enter_context(nc.Block())

            @block.sync
            def _(sp):
                def load_adj(b, k):
                    for hf in range(2):
                        free(sp, mask_ok, 2 * k + hf - 1)
                        free(sp, chk_ok, 2 * k + hf - 1)
                        sp.dma_start(adj_h[hf][:], adj[b, k * P:(k + 1) * P, hf * (N // 2):(hf + 1) * (N // 2)])\
                          .then_inc(adj_in[hf], 16)

                def load_hx(b, k):
                    free(sp, x1_ok, k - 3)
                    sp.dma_start(hx[k % 4][:, 0, :], table_g[b, k * P:(k + 1) * P, :]).then_inc(hx_in[k % 4], 16)
                    sp.dma_start(hx[k % 4][:, 1, :], x[b, k * P:(k + 1) * P, :]).then_inc(hx_in[k % 4], 16)

                def load_values(b, g):
                    free(sp, hpl_used, g - 1)
                    sp.dma_start(hpl[g % 2][:], hp_d[b, 2 * g:2 * g + 2].rearrange("t p c -> p t c"))\
                      .then_inc(hpl_in[g % 2], 16)

                def load_quarter(b, q):
                    free(sp, unit_done, (q - 1) * H)
                    sp.dma_start(maskq[q % 2][:], maskT_d[b, q * Q:(q + 1) * Q].rearrange("t p j r -> p t j r"))\
                      .then_inc(maskq_in[q % 2], 16)

                def load_unit(b, u):
                    q, h = u // H, u % H
                    free(sp, unit_done, u - 1)
                    sp.dma_start(srcb[h % 2][:], src_d[b, h, q * Q * P:(q + 1) * Q * P].partition_broadcast(P))\
                      .then_inc(srcb_in[h % 2], 16)
                    if h == 0:
                        free(sp, unit_done, u)
                        free(sp, out_st[q % 2], q // 2 * 16)
                        sp.dma_start(outq[q % 2][:], x1_d[b, q * Q:(q + 1) * Q].rearrange("t p c -> p t c")).then_inc(xh_in, 16)
                        sp.dma_start(hq[:], hp_d[b, q * Q:(q + 1) * Q].rearrange("t p c -> p t c")).then_inc(xh_in, 16)

                if b1 is not None:
                    load_adj(b1, 0)
                if b2 is not None:
                    for g in range(NT // 2):
                        load_values(b2, g)
                    load_quarter(b2, 0)
                for j in steps:
                    if b1 is not None and 1 <= j < NT:
                        load_adj(b1, j)
                    if b1 is not None and j < NT:
                        load_hx(b1, j)
                    if b2 is not None and 1 <= j <= NT:
                        load_unit(b2, j - 1)
                        if (j - 1) % H == 0 and j + H <= NT:
                            load_quarter(b2, (j - 1) // H + 1)

            @block.gpsimd
            def _(pool):
                if b1 is None:
                    return
                for k in range(NT):
                    pool.wait_ge(idx_ok, (k + 1))
                    for g in range(NR):
                        free(pool, red_ok, (k - 1) * NR + g + 1)
                        for s in range(RG):
                            pool.indirect_dma_start(
                                out=gath[g][:, s, :], out_offset=None, in_=table,
                                in_offset=bass.IndirectOffsetOnAxis(ap=idx[k % 2][:, g * RG + s:g * RG + s + 1], axis=0),
                            ).then_inc(g_in[g * RG + s], 16)
                for s in range(S):
                    pool.wait_ge(g_in[s], NT * 16)

            @block.vector
            def _(dve):
                v = nc.vector
                link = Chain(dve, dve_c).link

                def make_mask(b, k):
                    for hf in range(2):
                        m = 2 * k + hf
                        dve.wait_ge(adj_in[hf], (k + 1) * 16)
                        free(dve, turn_ok, m - 1)
                        v.tensor_scalar(mask_h[hf][:], adj_h[hf][:], 0.0, None, ALU.not_equal).then_inc(mask_ok, 1)

                def first_neighbours(b, k):
                    dve.wait_ge(keys_ok, (k + 1))
                    link(v.scalar_tensor_tensor(key[:], kps[:, 0:NG], 0.0, base[:], ALU.is_gt, ALU.mult))
                    link(v.tensor_tensor(key[:], key[:], kps[:, 0:NG], ALU.add))
                    for r in range(4):
                        link(v.max(k32[:, 8 * r:8 * r + 8], key[:]))
                        if r < 3:
                            link(v.match_replace(out=key[:], in_to_replace=k32[:, 8 * r:8 * r + 8], in_values=key[:],
                                                 imm_value=0.0))
                    link(v.tensor_copy(ki[:], k32[:, 0:S]))
                    link(v.tensor_scalar(b8[:], ki[:], 8, 3, ALU.logical_shift_right, ALU.logical_shift_left))
                    link(v.tensor_tensor(an[:], over(ki[:], 2, [P, S, GB]), bitc[:], ALU.bitwise_and))
                    link(v.tensor_tensor(sco[:], over(b8[:], 2, [P, S, GB]), ofsc[:], ALU.subtract))
                    link(v.scalar_tensor_tensor(cand[:], an[:].rearrange("p s g -> p (s g)"), 0.0,
                                                sco[:].rearrange("p s g -> p (s g)"), ALU.is_gt, ALU.mult))
                    for r in range(4):
                        link(v.max(c32[:, 8 * r:8 * r + 8], cand[:]))
                        if r < 3:
                            link(v.match_replace(out=cand[:], in_to_replace=c32[:, 8 * r:8 * r + 8], in_values=cand[:],
                                                 imm_value=0.0))
                    v.tensor_scalar(idx[k % 2][:], c32[:, 0:S], -1.0, rowbase[:, 0:1], ALU.mult, ALU.add)\
                     .then_inc(idx_ok, 1)

                def take_max(b, k, groups):
                    for g in groups:
                        for s in range(RG):
                            dve.wait_ge(g_in[g * RG + s], (k + 1) * 16)
                        v.tensor_reduce(part[:, g, :], gath[g][:].rearrange("p s c -> p c s"), AX_X, ALU.max)\
                         .then_inc(red_ok, 1)
                    if NR - 1 in groups:
                        dve.wait_ge(red_ok, (k + 1) * NR)
                        v.tensor_reduce(agg[:], part[:].rearrange("p g c -> p c g"), AX_X, ALU.max).then_inc(agg_ok, 1)

                def residual_norm(b, k):
                    dve.wait_ge(lin_ok, (k + 1))
                    free(dve, x1_out[k % 2], k // 2 * 16)
                    wait_hx(dve, b, k)
                    link(v.scalar_tensor_tensor(x1[k % 2][:], kps[:, NG:2 * NG], 0.0, hx[k % 4][:, 1, :],
                                                ALU.max, ALU.add))
                    dve.sem_inc(x1_ok, 1)
                    link(v.bn_stats(st1[:], x1[k % 2][:]))
                    v.bn_aggr(mv1[:], st1[:]).then_inc(var1_ok, 1)

                def norm_scale(b, k):
                    dve.wait_ge(root1_ok, k + 1)
                    link(v.reciprocal(rs1[:, 0:1], rs1[:, 0:1]))
                    v.scalar_tensor_tensor(rs1[:, 1:2], mv1[:, 0:1], -1.0, rs1[:, 0:1], ALU.mult, ALU.mult)\
                     .then_inc(ln1_ok, 1)

                def factors(b):
                    link(v.tensor_copy(sd2[:], sd[:]))
                    dve.sem_inc(sd_ok, 1)
                    s2, d2 = sd2[:, :, 0:H], sd2[:, :, H:2 * H]
                    link(v.tensor_scalar(negd[:], d2, -1.0, None, ALU.mult))
                    link(v.tensor_reduce(dmm[:, 0:H], d2.rearrange("p t h -> p h t"), AX_X, ALU.max))
                    v.tensor_reduce(dmm[:, H:2 * H], negd[:].rearrange("p t h -> p h t"), AX_X, ALU.max).then_inc(dd_ok, 1)
                    dve.wait_ge(dT_ps, 1)
                    link(v.tensor_reduce(drow[:], cps[0:2 * H, 0:P], AX_X, ALU.max))
                    v.tensor_scalar(ddiag[:], ident[0:2 * H, 0:2 * H], drow[:, 0:1], None, ALU.mult).then_inc(dd_ok, 1)
                    dve.wait_ge(db_ps, 1)
                    link(v.tensor_copy(dmax[:], cps[:, P:P + 2 * H]))
                    dmx = over(dmax[:, 0:H], 1, [P, NT, H])
                    v.tensor_tensor(tmpz[:], d2, dmx, ALU.subtract).then_inc(exp_in, 1)
                    link(v.tensor_tensor(tmpn[:], s2, dmx, ALU.add))
                    link(v.tensor_scalar(tmpp[:], tmpn[:], 0.0, None, ALU.max))
                    v.tensor_scalar(tmpn[:], tmpn[:], 0.0, None, ALU.min).then_inc(exp_in, 1)
                    dve.wait_ge(exp_ok, 4)

                def values(b):
                    for g in range(NT // 2):
                        t = slice(2 * g, 2 * g + 2)
                        dve.wait_ge(hpl_in[g % 2], (g // 2 + 1) * 16)
                        free(dve, val_ok, g)
                        hv = hpl[g % 2][:].rearrange("p t (h e) -> p (t h) e", h=H)
                        for i, e in enumerate((eB, eB1)):
                            ee = e[:, t, :].rearrange("p t h -> p (t h)")
                            v.tensor_tensor(vf[:, :, i * (E + 1):i * (E + 1) + E], hv, over(ee, 2, [P, 2 * H, E]), ALU.mult)
                            ins = v.tensor_copy(vf[:, :, i * (E + 1) + E], ee)
                        link(ins)
                        dve.sem_inc(hpl_used, 1)
                        o = val[:, 2 * g * H:(2 * g + 2) * H]
                        link(v.tensor_copy(o[:, :, 0, :], vf[:]))
                        link(v.tensor_tensor(vf[:], vf[:], o[:, :, 0, :], ALU.subtract))
                        link(v.tensor_copy(o[:, :, 1, :], vf[:]))
                        v.tensor_tensor(o[:, :, 2, :], vf[:], o[:, :, 1, :], ALU.subtract).then_inc(val_ok, 1)

                def unit_edges(b, q, h, tiles):
                    u = q * H + h
                    dve.wait_ge(srcb_in[h % 2], (q * (H // 2) + h // 2 + 1) * 16)
                    dve.wait_ge(maskq_in[q % 2], (q // 2 + 1) * 16)
                    for jt in tiles:
                        free(dve, gt_used, u * NT + jt - 3)
                        v.scalar_tensor_tensor(gt[jt % 4][:].rearrange("p (t r) -> p t r", t=Q),
                                               srcb[h % 2][:].rearrange("p (t r) -> p t r", t=Q), negd[:, jt, h:h + 1],
                                               maskq[q % 2][:, :, jt, :], ALU.is_gt, ALU.mult).then_inc(gt_ok, 1)

                def read_masked(b, q, h, pair):
                    u, w = q * H + h, K3 * (E + 1)
                    dve.wait_ge(macc_ok, 2 * u + pair + 1)
                    for i in range(2):
                        ins = v.tensor_reduce(ms[:, 2 * pair + i, :], macc[:, i * w:(i + 1) * w].rearrange(
                            "p (k v) -> p v k", k=K3), AX_X, ALU.add)
                    ins.then_inc(macc_used, 1)

                def unit_rows(b, q, h):
                    u = q * H + h
                    dve.wait_ge(gt_used, (u + 1) * NT)
                    for t in range(Q):
                        v.tensor_reduce(gs[:, t, :], acc[t][:, 0:K3 * V].rearrange("p (k v) -> p v k", k=K3), AX_X, ALU.add)\
                         .then_inc(acc_used, 1)
                    dve.wait_ge(macc_used, (2 * u + 2))
                    dve.wait_ge(acc_used, (u + 1) * Q)
                    rows = slice(q * Q, (q + 1) * Q)

                    def each(ap, n=E):
                        return over(ap, 2, [P, Q, n])

                    a, a1 = eA[:, rows, h], eA1[:, rows, h]
                    link(v.tensor_tensor(f0[:], ms[:], gs[:, :, E + 1:V], ALU.subtract))
                    v.tensor_tensor(f0[:], f0[:], each(a1, E + 1), ALU.mult)
                    link(v.tensor_tensor(gs[:, :, 0:E + 1], gs[:, :, 0:E + 1], each(a, E + 1), ALU.mult))
                    link(v.tensor_tensor(f0[:], f0[:], gs[:, :, 0:E + 1], ALU.add))
                    link(v.reciprocal(rden[:], f0[:, :, E]))
                    link(v.tensor_tensor(f1[:], f0[:, :, 0:E], each(rden[:]), ALU.mult))
                    link(v.tensor_tensor(f1[:], f1[:], over(bias_b[:, h, :], 1, [P, Q, E]), ALU.add))
                    dve.wait_ge(xh_in, (q + 1) * 32)
                    link(v.scalar_tensor_tensor(f1[:], f1[:], 0.0, hq[:, :, h * E:(h + 1) * E], ALU.max, ALU.add))
                    link(v.tensor_reduce(mean[:], f1[:], AX_X, ALU.add))
                    link(v.tensor_scalar(mean[:], mean[:], -1.0 / E, None, ALU.mult))
                    link(v.tensor_tensor(f1[:], f1[:], each(mean[:]), ALU.add))
                    link(v.tensor_tensor(f0[:, :, 0:E], f1[:], f1[:], ALU.mult))
                    v.tensor_reduce(var[:], f0[:, :, 0:E], AX_X, ALU.add).then_inc(var2_ok, 1)

                def unit_out(b, q, h):
                    def each(ap):
                        return over(ap, 2, [P, Q, E])

                    dve.wait_ge(root2_ok, q * H + h + 1)
                    link(v.reciprocal(var[:], var[:]))
                    link(v.tensor_tensor(f1[:], f1[:], each(var[:]), ALU.mult))
                    link(v.tensor_tensor(f1[:], f1[:], over(gamma_b[:, h, :], 1, [P, Q, E]), ALU.mult))
                    link(v.tensor_tensor(f1[:], f1[:], over(beta_b[:, h, :], 1, [P, Q, E]), ALU.add))
                    o = outq[q % 2][:, :, h * E:(h + 1) * E]
                    v.tensor_tensor(o, f1[:], o, ALU.add)\
                     .then_inc(unit_done, 1)


                if b2 is not None and b1 is None:
                    factors(b2)
                    values(b2)
                for j in steps:
                    one, layer, gather = b1 is not None and j < NT, b1 is not None and j >= 2, b1 is not None and 1 <= j <= NT
                    unit = ((j - 1) // H, (j - 1) % H) if b2 is not None and 1 <= j <= NT else None
                    for s in range(NT):
                        if s == 0 and one:
                            make_mask(b1, j)
                        if s == 0 and b2 is not None and 2 <= j <= NT + 1:
                            unit_out(b2, (j - 2) // H, (j - 2) % H)
                        if s == 5 and layer:
                            residual_norm(b1, j - 2)
                        if s == 7 and layer:
                            norm_scale(b1, j - 2)
                        if s == 7 and gather:
                            take_max(b1, j - 1, range(0, 1))
                        if s == 8 and gather:
                            take_max(b1, j - 1, range(1, 2))
                        if s == 9 and one:
                            first_neighbours(b1, j)
                        if s == 11 and gather:
                            take_max(b1, j - 1, range(2, 3))
                        if s == 13 and gather:
                            take_max(b1, j - 1, range(3, 4))
                        if s == 15 and gather:
                            take_max(b1, j - 1, range(4, 5))
                        if unit:
                            if s == 10:
                                read_masked(b2, *unit, 0)
                            unit_edges(b2, *unit, [s])
                    if unit:
                        read_masked(b2, *unit, 1)
                        unit_rows(b2, *unit)
                        if j == NT and b1 is None:
                            unit_out(b2, *unit)
                    if j == NT - 1 and one:
                        link(v.tensor_scalar(rowbase[:], rowbase[:], float(ROWS), None, ALU.add))
                    if j == 0 and both:
                        factors(b2)
                        values(b2)

            @block.tensor
            def _(pe):
                mm, turn = nc.tensor.matmul, nc.tensor.transpose

                def turn_activations(b, k):
                    pe.wait_ge(agg_ok, (k + 1))
                    if k == 0 and both:
                        pe.wait_ge(exp_in, 1)
                    wait_hx(pe, b, k)
                    free(pe, hp_ok, 3 * k)
                    for i in range(2):
                        turn(cps[:, i * P:(i + 1) * P], hx[k % 4][:, 0, i * P:(i + 1) * P], ident[:])
                    for i in range(2):
                        ins = turn(cps[:, (2 + i) * P:(3 + i) * P], agg[:, i * P:(i + 1) * P], ident[:])
                    ins.then_inc(hT_ps, 1)

                def turn_mask(b, k, hf):
                    m = 2 * k + hf
                    pe.wait_ge(mask_ok, m + 1)
                    free(pe, mT_ok, m)
                    for i in range(NT // 2):
                        ins = turn(tps[:, i * P:(i + 1) * P], mask_h[hf][:, i * P:(i + 1) * P], identb[:])
                    ins.then_inc(turn_ok, 1)

                def dense0(b, k):
                    pe.wait_ge(hT_ok, (k + 1))
                    free(pe, x1_ok, k)
                    free(pe, idx_ok, min(k + 2, NT))
                    o = kps[:, NG:2 * NG]
                    for i in range(4):
                        mm(o, hT[:, i, :], w0_sb[:, i, :], start=(i == 0), stop=False)
                    mm(o, ones[0:1, :], b0_sb[:], start=False, stop=True).then_inc(lin_ok, 1)

                def group_bytes(b, k):
                    free(pe, x1_ok, k - 1)
                    pe.wait_ge(mT_ok, (2 * k + 2))
                    free(pe, idx_ok, k)
                    for t in range(NT):
                        ins = mm(kps[:, t * GPT:(t + 1) * GPT], mT[k % 2][:, t, :], bits_w[:], start=True, stop=True)
                    ins.then_inc(keys_ok, 1)

                def turn_h1(b, k):
                    pe.wait_ge(h1_ok, (k + 1))
                    for i in range(2):
                        ins = turn(cps[:, i * P:(i + 1) * P], h1[:, i * P:(i + 1) * P], ident[:])
                    ins.then_inc(h1T_ps, 1)

                def project1(b, k):
                    pe.wait_ge(h1T_ok, (k + 1))
                    for i in range(2):
                        mm(cps[:, 0:W1N], h1T[:, i, :], r1[:, i, :], start=(i == 0), stop=(i == 1))
                    for i in range(2):
                        ins = mm(cps[0:H, 3 * P:4 * P], r1[:, i, C:C + H], h1T[:, i, :], start=(i == 0), stop=(i == 1))
                    ins.then_inc(hp_ps, 1)

                def factors(b):
                    pe.wait_ge(dd_ok, 1)
                    turn(cps[0:2 * H, 0:P], dmm[:], ident[:]).then_inc(dT_ps, 1)
                    pe.wait_ge(dd_ok, 2)
                    mm(cps[:, P:P + 2 * H], ones[0:2 * H, :], ddiag[:], start=True, stop=True).then_inc(db_ps, 1)

                def unit_edges(b, q, h, jt):
                    u = q * H + h
                    if u == 0 and jt == 0:
                        pe.wait_ge(val_ok, NT // 2)
                    pe.wait_ge(gt_ok, u * NT + jt + 1)
                    for t in range(Q):
                        if jt == 0:
                            free(pe, acc_used, (u - 1) * Q + t + 1)
                        ins = mm(acc[t][:, 0:K3 * V], gt[jt % 4][:, t * P:(t + 1) * P],
                                 val[:, jt * H + h].rearrange("p k v -> p (k v)"), start=(jt == 0), stop=(jt == NT - 1))
                    ins.then_inc(gt_used, 1)

                def unit_masked(b, q, h, pair, part_of):
                    u, w = q * H + h, K3 * (E + 1)
                    if part_of == 0:
                        pe.wait_ge(maskq_in[q % 2], (q // 2 + 1) * 16)
                        if u == 0:
                            pe.wait_ge(val_ok, NT // 2)
                        free(pe, macc_used, 2 * u + pair)
                    i = part_of // 2
                    for jt in range(part_of % 2 * (NT // 2), (part_of % 2 + 1) * (NT // 2)):
                        ins = mm(macc[:, i * w:(i + 1) * w], maskq[q % 2][:, 2 * pair + i, jt, :],
                                 val[:, jt * H + h, :, E + 1:V], start=(jt == 0), stop=(jt == NT - 1))
                    if part_of == 3:
                        ins.then_inc(macc_ok, 1)


                if b2 is not None and b1 is None:
                    factors(b2)
                for j in steps:
                    one, layer = b1 is not None and j < NT, b1 is not None and j >= 2
                    unit = ((j - 1) // H, (j - 1) % H) if b2 is not None and 1 <= j <= NT else None
                    for s in range(NT):
                        if s == 0 and layer:
                            turn_activations(b1, j - 2)
                        if s == 1 and one:
                            turn_mask(b1, j, 0)
                        if s == 3 and layer:
                            dense0(b1, j - 2)
                        if s == 4 and one:
                            turn_mask(b1, j, 1)
                        if s == 7 and one:
                            group_bytes(b1, j)
                        if s == 9 and layer:
                            turn_h1(b1, j - 2)
                        if s == 11 and layer:
                            project1(b1, j - 2)
                        if unit:
                            if 4 <= s < 8:
                                unit_masked(b2, *unit, 0, s - 4)
                            if 12 <= s < 16:
                                unit_masked(b2, *unit, 1, s - 12)
                            unit_edges(b2, *unit, s)
                    if j == 0 and both:
                        factors(b2)

            @block.scalar
            def _(act):
                a = nc.scalar

                def activations_out(b, k):
                    act.wait_ge(hT_ps, (k + 1))
                    a.copy(hT[:].rearrange("p i r -> p (i r)"), cps[:]).then_inc(hT_ok, 1)

                def mask_out(b, k, hf):
                    m = 2 * k + hf
                    act.wait_ge(adj_in[hf], (k + 1) * 16)
                    free(act, chk_ok, m)
                    a.activation(sq[:], adj_h[hf][:], ACT.Square, bias=mhalf[:, 0:1], accum_out=chk[:, m:m + 1]).then_inc(chk_ok, 1)
                    act.wait_ge(turn_ok, m + 1)
                    if hf == 0:
                        free(act, mT_out[k % 2], k // 2 * 16)
                    a.copy(mT[k % 2][:, hf * (NT // 2):(hf + 1) * (NT // 2), :].rearrange("p t r -> p (t r)"), tps[:])\
                     .then_inc(mT_ok, 1)
                    if hf == 1:
                        act.wait_ge(mT_ok, (m + 1))
                        act.dma_start(maskT_d[b, k], mT[k % 2][:]).then_inc(mT_out[k % 2], 16)

                def root1(b, k):
                    act.wait_ge(var1_ok, k + 1)
                    a.activation(rs1[:, 0:1], mv1[:, 1:2], ACT.Sqrt, bias=epsc[:, 0:1]).then_inc(root1_ok, 1)

                def root2(b, u):
                    act.wait_ge(var2_ok, u + 1)
                    a.activation(var[:], var[:], ACT.Sqrt, bias=epsc[:, 1:2], scale=1.0 / E).then_inc(root2_ok, 1)

                def normalise(b, k):
                    act.wait_ge(ln1_ok, (k + 1))
                    act.dma_start(x1_d[b, k], x1[k % 2][:]).then_inc(x1_out[k % 2], 16)
                    a.activation(h1[:], x1[k % 2][:], ACT.Relu, bias=rs1[:, 1:2], scale=rs1[:, 0:1]).then_inc(h1_ok, 1)

                def h1_out(b, k):
                    act.wait_ge(h1T_ps, (k + 1))
                    a.copy(h1T[:].rearrange("p i r -> p (i r)"), cps[:, 0:2 * P]).then_inc(h1T_ok, 1)

                def projected_out(b, k):
                    act.wait_ge(hp_ps, (k + 1))
                    free(act, hp_out[k % 2], k // 2 * 16)
                    free(act, e_out[k % 2], k // 2 * 16)
                    if k == 0 and both:
                        act.wait_ge(sd_ok, 1)
                    a.copy(hps[k % 2][:], cps[:, 0:C]).then_inc(hp_ok, 1)
                    a.copy(sd[:, k, :], cps[:, C:W1N]).then_inc(hp_ok, 1)
                    a.copy(eT[k % 2][:], cps[0:H, 3 * P:4 * P]).then_inc(hp_ok, 1)
                    act.wait_ge(hp_ok, 3 * (k + 1))
                    act.dma_start(hp_d[b, k], hps[k % 2][:]).then_inc(hp_out[k % 2], 16)
                    act.dma_start(src_d[b, :, k * P:(k + 1) * P], eT[k % 2][:]).then_inc(e_out[k % 2], 16)

                def factors(b):
                    act.wait_ge(exp_in, 1)
                    a.activation(eB[:], tmpz[:], ACT.Exp).then_inc(exp_ok, 1)
                    a.activation(eB1[:], tmpz[:], ACT.Exp, scale=SLOPE).then_inc(exp_ok, 1)
                    act.wait_ge(exp_in, 2)
                    a.activation(eA[:], tmpn[:], ACT.Exp, scale=1.0 - SLOPE).then_inc(exp_ok, 1)
                    a.activation(eA1[:], tmpp[:], ACT.Exp, scale=SLOPE - 1.0).then_inc(exp_ok, 1)

                def store_out(b, q):
                    act.wait_ge(unit_done, (q + 1) * H)
                    act.dma_start(out[b, q * Q * P:(q + 1) * Q * P, :].rearrange("(t p) c -> p t c", p=P), outq[q % 2][:])\
                       .then_inc(out_st[q % 2], 16)


                if b2 is not None and b1 is None:
                    factors(b2)
                for j in steps:
                    one, layer = b1 is not None and j < NT, b1 is not None and j >= 2
                    if layer:
                        activations_out(b1, j - 2)
                    if one:
                        mask_out(b1, j, 0)
                        mask_out(b1, j, 1)
                    if layer:
                        root1(b1, j - 2)
                        normalise(b1, j - 2)
                        h1_out(b1, j - 2)
                        projected_out(b1, j - 2)
                    if j == 0 and both:
                        factors(b2)
                    if b2 is not None and 1 <= j <= NT:
                        root2(b2, j - 1)
                    if b2 is not None and j >= 2 and (j - 2) % H == H - 1:
                        store_out(b2, (j - 2) // H)
                if b2 is not None and b1 is None:
                    store_out(b2, NQ - 1)
                if b1 is not None:
                    for s in mT_out + x1_out + hp_out + e_out:
                        act.wait_ge(s, NT // 2 * 16)
                if b2 is not None:
                    for s in out_st:
                        act.wait_ge(s, NQ // 2 * 16)

        with ExitStack() as turns:
            turn_of_engines(0, None)
        reset()
        with nc.Fori(0, B - 1) as b:
            with ExitStack() as turns:
                turn_of_engines(b + 1, b)
            reset()
        with ExitStack() as turns:
            turn_of_engines(None, B - 1)


def constants():
    i = np.arange(P)
    bits = np.where(i[:, None] // GB == np.arange(GPT)[None, :], 1 << (i[:, None] % GB), 0)
    g = np.arange(NG)
    b = np.broadcast_to(np.arange(GB), (P, S, GB))
    return {
        "c_ident": np.eye(P, dtype=np.float32),
        "c_bits": bits.astype(mybir.dt.np(BF16)),
        "c_base": np.broadcast_to((256 * (NG - g)).astype(np.float32), (P, NG)).copy(),
        "c_bit": (1 << b).astype(np.int32),
        "c_ofs": b.astype(np.int32),
    }


_INS = ["x", "adj", "L0_gnn_W", "L0_gnn_b", "L1_gnn_W", "L1_gnn_a_src", "L1_gnn_a_dst", "L1_gnn_bias",
        "L1_gnn_ln_gamma", "L1_gnn_ln_beta"]


def kernel(**inputs):
    import concourse.bacc as bacc
    from concourse.bass_utils import run_bass_kernel_spmd

    nc = bacc.Bacc("TRN2", target_bir_lowering=False, num_devices=1)
    arrays, args = {}, []
    for name, a in [(n, inputs[n]) for n in _INS] + list(constants().items()):
        a = np.ascontiguousarray(a)
        arrays[name] = a
        args.append(nc.dram_tensor(name, a.shape, mybir.dt.from_np(a.dtype), kind="ExternalInput").ap())
    args.append(nc.dram_tensor("out", (B, N, C), F32, kind="ExternalOutput").ap())
    graph_layers(nc, *args)
    r = run_bass_kernel_spmd(nc, [arrays], core_ids=[0])
    return r.results[0]["out"]
```

```python
from contextlib import ExitStack

import numpy as np

import concourse.bass as bass
from concourse import mybir

ALU = mybir.AluOpType
ACT = mybir.ActivationFunctionType
AX_X = mybir.AxisListType.X
F32 = mybir.dt.float32
BF16 = mybir.dt.bfloat16
I32 = mybir.dt.int32
U32 = mybir.dt.uint32

P = 128
B, N, C = 8, 2048, 256
S = 25
H, E = 4, 64
T = 5
NT = N // P
EPS0 = 1e-5
EPS1 = 1e-6
NEG = -1.0e9
SLOPE = 0.01
ROWS = N + 1
GB = 8
NG = N // GB
GPT = P // GB
GROUPS = (range(0, 12), range(12, S))
NR = len(GROUPS)
V = 2 * E + 2
K3 = 3
BIG = 2.0 ** 64
RANGE = 60.0
Q = 4
NQ = NT // Q
D = 6
AHEAD, BEHIND = 2, 2


class Chain:

    count = {}

    def __init__(self, eng, sem, fresh=False):
        self.eng, self.sem, self.last = eng, sem, 0
        if fresh:
            Chain.count[sem.num] = 0

    def done(self, ins):
        Chain.count[self.sem.num] += 1
        self.last = Chain.count[self.sem.num]
        ins.then_inc(self.sem, 1)

    def ready(self):
        free(self.eng, self.sem, self.last)

    def link(self, ins):
        self.done(ins)
        self.ready()


def free(eng, sem, n):
    if n > 0:
        eng.wait_ge(sem, n)


def over(ap, axis, shape):
    return ap.unsqueeze(axis).to_broadcast(shape)


def graph_layers(nc, x, adj, w0, b0, w1, a_src, a_dst, bias1, gamma1, beta1, c_ident, c_bits, c_base, c_bit, c_ofs, out):
    with ExitStack() as ctx:
        fast = ExitStack()
        owner = [ctx]

        def sb(name, shape, dt=F32):
            return owner[-1].enter_context(nc.sbuf_tensor(name, shape, dt))

        def ps(name, shape, dt=F32):
            return owner[-1].enter_context(nc.psum_tensor(name, shape, dt))

        sems = []

        def sem(name):
            sems.append(ctx.enter_context(nc.semaphore(name)))
            return sems[-1]

        def reset():
            ids = sorted(s.num for s in sems)
            assert ids == list(range(ids[0], ids[-1] + 1))
            nc.gpsimd.dma_reset(range(ids[0], ids[-1] + 1))
            nc.gpsimd.sem_clear(range(ids[0], ids[-1] + 1))
            nc.all_engine_barrier()

        def scratch(name, shape, dt=F32):
            return nc.dram_tensor(name, shape, dt, kind="Internal").ap()

        table = scratch("table", (B * ROWS, C))
        maskT_d = scratch("maskT_d", (B, NT, P, NT, P), BF16)
        x1_d = scratch("x1_d", (B, NT, P, C))
        hp_d = scratch("hp_d", (B, NT, P, C))
        src_d = scratch("src_d", (B, H, N))
        table_g = table.rearrange("(b r) c -> b r c", b=B)

        ident = sb("ident", [P, P])
        identb = sb("identb", [P, P], BF16)
        good = sb("good", [P, 4])
        gsum, gsum_i = sb("gsum", [1, 1]), sb("gsum_i", [1, 1], I32)
        bits_w = sb("bits_w", [P, GPT], BF16)
        base = sb("base", [P, NG])
        bitc = sb("bitc", [P, GB], I32)
        ofsc = sb("ofsc", [P, GB], I32)
        ones = sb("ones", [P, P])
        w0_sb = sb("w0_sb", [P, 4, C])
        b0_sb = sb("b0_sb", [1, C])
        r1 = sb("r1", [P, 2, C + 2 * H])
        bias_b = sb("bias_b", [P, H, E])
        gamma_b = sb("gamma_b", [P, H, E])
        beta_b = sb("beta_b", [P, H, E])
        zero_b = sb("zero_b", [B, C])
        mhalf = sb("mhalf", [P, 1])
        epsc = sb("epsc", [P, 2])

        owner.append(fast)
        x0 = [sb(f"x0_{i}", [P, Q, C]) for i in range(2)]
        st0 = sb("st0", [P, Q, 6])
        mv0 = sb("mv0", [P, Q, 2])
        rs0 = [sb(f"rs0_{i}", [P, Q]) for i in range(2)]
        nm0 = [sb(f"nm0_{i}", [P, Q]) for i in range(2)]

        adj_h = [sb(f"adj_h{i}", [P, N // 2], I32) for i in range(2)]
        mask_h = [sb(f"mask_h{i}", [P, N // 2], BF16) for i in range(2)]
        sq = sb("sq", [P, N // 2], BF16)
        gtmp = sb("gtmp", [P, H])
        degmin = sb("degmin", [P, 1])
        chk = sb("chk", [P, 2 * NT])
        mT = [sb(f"mT{i}", [P, NT, P], BF16) for i in range(2)]
        key = sb("key", [P, NG])
        k32 = sb("k32", [P, 32])
        ki = sb("ki", [P, S], I32)
        b8 = sb("b8", [P, S], I32)
        an = sb("an", [P, S, GB], I32)
        cand = sb("cand", [P, S * GB])
        c32 = sb("c32", [P, 32])
        rowbase = sb("rowbase", [P, 1])
        idx = [sb(f"idx{i}", [P, S], U32) for i in range(2)]
        gath = [sb(f"gath{g}", [P, len(GROUPS[g]), C]) for g in range(NR)]
        part = sb("part", [P, NR, C])
        hx = [sb(f"hx{i}", [P, 2, C]) for i in range(4)]
        agg = sb("agg", [P, C])
        hT = sb("hT", [P, 4, P])
        x1 = [hx[i][:, 1, :] for i in range(4)]
        st1 = sb("st1", [P, 6])
        mv1 = sb("mv1", [P, 2])
        rs1 = sb("rs1", [P, 2])
        h1 = sb("h1", [P, C])
        h1T = sb("h1T", [P, 2, P])
        hps = [sb(f"hps{i}", [P, C]) for i in range(2)]
        sd = sb("sd", [P, NT, 2 * H])
        eT = [sb(f"eT{i}", [H, P]) for i in range(2)]

        sd2 = sb("sd2", [P, NT, 2 * H])
        dmm = sb("dmm", [P, 2 * H])
        drow = sb("drow", [2 * H, 1])
        ddiag = sb("ddiag", [2 * H, 2 * H])
        dmax = sb("dmax", [P, 2 * H])
        tmpz = sb("tmpz", [P, NT, H])
        tmpn = sb("tmpn", [P, NT, H])
        tmpp = sb("tmpp", [P, NT, H])
        negd = sb("negd", [P, NT, H])
        eB = sb("eB", [P, NT, H])
        eB1 = sb("eB1", [P, NT, H])
        eA = sb("eA", [P, NT, H])
        eA1 = sb("eA1", [P, NT, H])
        flat = sb("flat", [P, Q * K3 * V])
        vf = flat[:, 0:2 * H * V].rearrange("p (a v) -> p a v", v=V)
        araw = flat[:].rearrange("p (t k v) -> p t k v", t=Q, k=K3)
        mraw = sb("mraw", [P, Q, K3, E + 1])
        kd = sb("kd", [P, NT, H])
        asrc, adst, wa_tmp = (flat[:, i * C:(i + 1) * C].rearrange("p (h e) -> p h e", h=H) for i in range(3))
        val = sb("val", [P, NT * H, K3, V], BF16)
        maskq = [sb(f"maskq{i}", [P, Q, NT, P], BF16) for i in range(2)]
        srcb = [sb(f"srcb{i}", [P, Q * P]) for i in range(2)]
        gt = [sb(f"gt{i}", [P, Q * P], BF16) for i in range(D)]
        rb = [sb(f"rb{i}", [P, Q * P], BF16) for i in range(D)]
        hq = sb("hq", [P, Q, C])
        hpl = [hq[:, 2 * i:2 * i + 2, :] for i in range(2)]
        gs, ms = araw[:, :, 0, :], mraw[:, :, 0, :]
        f0 = sb("f0", [P, Q, E + 1])
        f1 = sb("f1", [P, Q, E])
        rden = sb("rden", [P, Q])
        msum = sb("msum", [P, Q])
        negm = sb("negm", [P, Q])
        var = sb("var", [P, Q])
        nm2 = sb("nm2", [P, Q])
        outq = x0

        acc = [ps(f"acc{i}", [P, 512]) for i in range(Q)]
        macc = ps("macc", [P, 512])
        tps = ps("tps", [P, 1024], BF16)
        kps = ps("kps", [P, 512])
        cps = ps("cps", [P, 512])

        owner.pop()

        const_in, const_ok = sem("const_in"), sem("const_ok")
        r1_ok = sem("r1_ok")
        dve_c = sem("dve_c")
        x0_in = [sem(f"x0_in{i}") for i in range(2)]
        x0_var, x0_root, x0_norm, x0_relu = sem("x0_var"), sem("x0_root"), sem("x0_norm"), sem("x0_relu")
        var1_ok, root1_ok, root2_ok = sem("var1_ok"), sem("root1_ok"), sem("root2_ok")
        x0_out = [sem(f"x0_out{i}") for i in range(2)]
        zero_out = sem("zero_out")
        adj_in = [sem(f"adj_in{i}") for i in range(2)]
        hx_in = [sem(f"hx_in{i}") for i in range(4)]
        mask_ok, chk_ok = sem("mask_ok"), sem("chk_ok")
        turn_ok, mT_ok, keys_ok, idx_ok = sem("turn_ok"), sem("mT_ok"), sem("keys_ok"), sem("idx_ok")
        g_in = [sem(f"g_in{s}") for s in range(S)]
        red_ok, agg_ok = sem("red_ok"), sem("agg_ok")
        hT_ps, hT_ok, lin_ok, x1_ok, ln1_ok, h1_ok = (sem("hT_ps"), sem("hT_ok"), sem("lin_ok"), sem("x1_ok"),
                                                      sem("ln1_ok"), sem("h1_ok"))
        h1T_ps, h1T_ok, hp_ps, hp_ok = sem("h1T_ps"), sem("h1T_ok"), sem("hp_ps"), sem("hp_ok")
        mT_out = [sem(f"mT_out{i}") for i in range(2)]
        x1_out = [sem(f"x1_out{i}") for i in range(4)]
        hp_out = [sem(f"hp_out{i}") for i in range(2)]
        e_out = [sem(f"e_out{i}") for i in range(2)]
        sd_ok = sem("sd_ok")
        dT_ps, dd_ok, db_ps, exp_in, exp_ok = sem("dT_ps"), sem("dd_ok"), sem("db_ps"), sem("exp_in"), sem("exp_ok")
        hpl_in = [sem(f"hpl_in{i}") for i in range(2)]
        val_ok = sem("val_ok")
        maskq_in = [sem(f"maskq_in{i}") for i in range(2)]
        srcb_in = [sem(f"srcb_in{i}") for i in range(2)]
        hq_in, xq_in, relu_ok, hq_used = sem("hq_in"), sem("xq_in"), sem("relu_ok"), sem("hq_used")
        bytes_ok, araw_ok, araw_used, mraw_ok, mraw_used = (sem("bytes_ok"), sem("araw_ok"), sem("araw_used"),
                                                            sem("mraw_ok"), sem("mraw_used"))
        msum_ok, negm_ok, sq2_ok, nm2_ok, app_ok = (sem("msum_ok"), sem("negm_ok"), sem("sq2_ok"),
                                                           sem("nm2_ok"), sem("app_ok"))
        gt_ok, gt_used = sem("gt_ok"), sem("gt_used")
        macc_ok = sem("macc_ok")
        unit_done = sem("unit_done")
        out_st = [sem(f"out_st{i}") for i in range(2)]

        good_ps, good_ok, gen_in, gen_out, sg_ok, dT_t, dT_ok = (sem("good_ps"), sem("good_ok"), sem("gen_in"), sem("gen_out"),
                                                                 sem("sg_ok"), sem("dT_t"), sem("dT_ok"))
        row_in, dst_in, dst_used, w_ok, p_ok = (sem("row_in"), [sem(f"dst_in{i}") for i in range(2)], sem("dst_used"),
                                                sem("w_ok"), sem("p_ok"))
        pT_ps, pT_ok, o_ps, mv_ok, root_ok, head_ok = (sem("pT_ps"), sem("pT_ok"), sem("o_ps"), sem("mv_ok"),
                                                       sem("root_ok"), sem("head_ok"))

        W1N = C + 2 * H
        STEPS = NT + 4

        with nc.Block() as block:
            @block.sync
            def _(sp):
                def row_bc(a, n):
                    return a.rearrange("h e -> (h e)").partition_broadcast(n)

                for dst, src in ((ident[:], c_ident), (base[:], c_base), (bitc[:], c_bit), (ofsc[:], c_ofs),
                                 (bits_w[:], c_bits), (w0_sb[:], w0.rearrange("(k p) o -> p k o", p=P)),
                                 (b0_sb[:], b0.unsqueeze(0)),
                                 (bias_b[:].rearrange("p h e -> p (h e)"), row_bc(bias1, P)),
                                 (gamma_b[:].rearrange("p h e -> p (h e)"), row_bc(gamma1, P)),
                                 (beta_b[:].rearrange("p h e -> p (h e)"), row_bc(beta1, P)),
                                 (asrc, a_src[:, 0, :].partition_broadcast(P)),
                                 (adst, a_dst[:, 0, :].partition_broadcast(P))):
                    sp.dma_start(dst, src).then_inc(const_in, 16)
                for k in range(2):
                    sp.dma_start(r1[:, k, 0:C].rearrange("p (h e) -> p h e", h=H),
                                 w1[:, k * P:(k + 1) * P, :].rearrange("h p e -> p h e")).then_inc(const_in, 16)
                sp.wait_ge(const_ok, 2)
                sp.dma_start(table_g[:, N, :], zero_b[:]).then_inc(zero_out, 16)


                sp.wait_ge(zero_out, 16)

            @block.vector
            def _(dve):
                v = nc.vector
                link = Chain(dve, dve_c, fresh=True).link
                v.memset(ones[:], 1.0).then_inc(const_ok, 1)
                link(v.memset(rowbase[:], float(N)))
                v.memset(zero_b[:], 0.0).then_inc(const_ok, 1)
                v.memset(mhalf[:], -0.5)
                v.memset(good[:], 1.0)
                v.memset(epsc[:, 0:1], EPS0)
                v.memset(epsc[:, 1:2], EPS1).then_inc(const_ok, 1)
                dve.wait_ge(const_in, 16 * 14)
                v.tensor_copy(identb[:], ident[:]).then_inc(const_ok, 1)
                for k in range(2):
                    w = r1[:, k, 0:C].rearrange("p (h e) -> p h e", h=H)
                    for j, a in enumerate((asrc, adst)):
                        link(v.tensor_tensor(wa_tmp, w, a, ALU.mult))
                        link(v.tensor_reduce(r1[:, k, C + H * j:C + H * j + H], wa_tmp, AX_X, ALU.add))
                dve.sem_inc(r1_ok, 1)


        reset()

        with nc.Fori(0, B) as b:
            with nc.Block() as block:
                @block.sync
                def _(sp):
                    for q in range(NQ):
                        free(sp, x0_out[q % 2], q // 2 * 16)
                        sp.dma_start(x0[q % 2][:], x[b, q * Q * P:(q + 1) * Q * P, :].rearrange("(t p) c -> p t c", p=P))\
                          .then_inc(x0_in[q % 2], 16)

                @block.vector
                def _(dve):
                    v = nc.vector
                    link = Chain(dve, dve_c, fresh=True).link
                    for q in range(NQ):
                        dve.wait_ge(x0_in[q % 2], (q // 2 + 1) * 16)
                        for t in range(Q):
                            ins = v.bn_stats(st0[:, t, :], x0[q % 2][:, t, :])
                        link(ins)
                        for t in range(Q):
                            ins = v.bn_aggr(mv0[:, t, :], st0[:, t, :])
                        link(ins)
                        ins = v.tensor_copy(rs0[q % 2][:], mv0[:, :, 1])
                        ins.then_inc(x0_var, 1)
                        dve.wait_ge(x0_root, q + 1)
                        link(v.reciprocal(rs0[q % 2][:], rs0[q % 2][:]))
                        v.scalar_tensor_tensor(nm0[q % 2][:], mv0[:, :, 0], -1.0, rs0[q % 2][:], ALU.mult, ALU.mult)\
                         .then_inc(x0_norm, 1)

                @block.scalar
                def _(act):
                    for q in range(NQ):
                        act.wait_ge(x0_var, q + 1)
                        nc.scalar.activation(rs0[q % 2][:], rs0[q % 2][:], ACT.Sqrt, bias=epsc[:, 0:1]).then_inc(x0_root, 1)
                        act.wait_ge(x0_norm, q + 1)
                        for t in range(Q):
                            nc.scalar.activation(x0[q % 2][:, t, :], x0[q % 2][:, t, :], ACT.Relu,
                                                 bias=nm0[q % 2][:, t:t + 1], scale=rs0[q % 2][:, t:t + 1])\
                              .then_inc(x0_relu, 1)
                        act.wait_ge(x0_relu, (q + 1) * Q)
                        act.dma_start(table_g[b, q * Q * P:(q + 1) * Q * P, :].rearrange("(t p) c -> p t c", p=P),
                                      x0[q % 2][:]).then_inc(x0_out[q % 2], 16)
                    for i in range(2):
                        act.wait_ge(x0_out[i], NQ // 2 * 16)
            reset()

        def wait_hx(eng, k):
            eng.wait_ge(hx_in[k % 4], (k // 4 + 1) * 32)

        def turn_of_engines(b1, b2):
            both = b1 is not None and b2 is not None
            block = turns.enter_context(nc.Block())

            def in_one(k):
                return b1 is not None and 0 <= k < NT

            def in_two(u):
                return b2 is not None and 0 <= u < NQ * H

            @block.sync
            def _(sp):
                def load_adj(b, k):
                    for hf in range(2):
                        free(sp, mask_ok, 2 * k + hf - 1)
                        free(sp, chk_ok, 2 * k + hf - 1)
                        sp.dma_start(adj_h[hf][:], adj[b, k * P:(k + 1) * P, hf * (N // 2):(hf + 1) * (N // 2)])\
                          .then_inc(adj_in[hf], 16)

                def load_hx(b, k):
                    free(sp, x1_out[k % 4], k // 4 * 16)
                    free(sp, h1_ok, k - 3)
                    sp.dma_start(hx[k % 4][:, 0, :], table_g[b, k * P:(k + 1) * P, :]).then_inc(hx_in[k % 4], 16)
                    sp.dma_start(hx[k % 4][:, 1, :], x[b, k * P:(k + 1) * P, :]).then_inc(hx_in[k % 4], 16)

                def load_values(b, g):
                    free(sp, val_ok, g - 1)
                    sp.dma_start(hpl[g % 2], hp_d[b, 2 * g:2 * g + 2].rearrange("t p c -> p t c"))\
                      .then_inc(hpl_in[g % 2], 16)

                def load_mask_quarter(b, q):
                    free(sp, gt_used, (q - 1) * H * NT)
                    sp.dma_start(maskq[q % 2][:], maskT_d[b, q * Q:(q + 1) * Q].rearrange("t p j r -> p t j r"))\
                      .then_inc(maskq_in[q % 2], 16)

                def load_src(b, u):
                    q, h = u // H, u % H
                    free(sp, relu_ok, (u - 1) * NT)
                    sp.dma_start(srcb[h % 2][:], src_d[b, h, q * Q * P:(q + 1) * Q * P].partition_broadcast(P))\
                      .then_inc(srcb_in[h % 2], 16)

                def load_rows(b, q):
                    free(sp, out_st[q % 2], q // 2 * 16)
                    sp.dma_start(outq[q % 2][:], x1_d[b, q * Q:(q + 1) * Q].rearrange("t p c -> p t c")).then_inc(xq_in, 16)
                    sp.wait_ge(val_ok, NT // 2)
                    free(sp, hq_used, q * H)
                    sp.dma_start(hq[:], hp_d[b, q * Q:(q + 1) * Q].rearrange("t p c -> p t c")).then_inc(hq_in, 16)

                for j in range(STEPS):
                    if in_one(j):
                        load_adj(b1, j)
                        load_hx(b1, j)
                    if j == 0 and b2 is not None:
                        for g in range(NT // 2):
                            load_values(b2, g)
                        load_mask_quarter(b2, 0)
                    if in_two(j):
                        load_src(b2, j)
                    if in_two(j - 1) and (j - 1) % H == 0:
                        load_rows(b2, (j - 1) // H)
                        if in_two(j - 1 + H):
                            load_mask_quarter(b2, (j - 1) // H + 1)

            @block.gpsimd
            def _(pool):
                if b1 is None:
                    return
                for k in range(NT):
                    pool.wait_ge(idx_ok, k + 1)
                    for g in range(NR):
                        free(pool, red_ok, 2 * ((k - 1) * NR + g + 1) if k else 0)
                        for i, s in enumerate(GROUPS[g]):
                            pool.indirect_dma_start(
                                out=gath[g][:, i, :], out_offset=None, in_=table,
                                in_offset=bass.IndirectOffsetOnAxis(ap=idx[k % 2][:, s:s + 1], axis=0),
                            ).then_inc(g_in[s], 16)
                for s in range(S):
                    pool.wait_ge(g_in[s], NT * 16)

            @block.vector
            def _(dve):
                v = nc.vector
                link = Chain(dve, dve_c, fresh=True).link
                top, rows, norm = Chain(dve, dve_c), Chain(dve, dve_c), Chain(dve, dve_c)

                def make_mask(k, hf):
                    m = 2 * k + hf
                    dve.wait_ge(adj_in[hf], (k + 1) * 16)
                    free(dve, turn_ok, m - 1)
                    v.tensor_scalar(mask_h[hf][:], adj_h[hf][:], 0.0, None, ALU.not_equal).then_inc(mask_ok, 1)

                def first_neighbours(k, piece):
                    top.ready()
                    if piece == 0:
                        dve.wait_ge(keys_ok, k + 1)
                        top.done(v.scalar_tensor_tensor(key[:], kps[:, 0:NG], 0.0, base[:], ALU.is_gt, ALU.mult))
                    elif piece == 1:
                        v.tensor_tensor(key[:], key[:], kps[:, 0:NG], ALU.add).then_inc(bytes_ok, 1)
                        dve.wait_ge(bytes_ok, k + 1)
                    elif piece < 9:
                        r, replace = divmod(piece - 2, 2)
                        eight = k32[:, 8 * r:8 * r + 8]
                        if replace:
                            top.done(v.match_replace(out=key[:], in_to_replace=eight, in_values=key[:], imm_value=0.0))
                        else:
                            top.done(v.max(eight, key[:]))
                    elif piece == 9:
                        top.done(v.tensor_copy(ki[:], k32[:, 0:S]))
                    elif piece == 10:
                        v.tensor_scalar(b8[:], ki[:], 8, 3, ALU.logical_shift_right, ALU.logical_shift_left)
                        top.done(v.tensor_tensor(an[:], over(ki[:], 2, [P, S, GB]), over(bitc[:], 1, [P, S, GB]), ALU.bitwise_and))
                    elif piece == 11:
                        top.done(v.tensor_tensor(cand[:].rearrange("p (s g) -> p s g", s=S), over(b8[:], 2, [P, S, GB]), over(ofsc[:], 1, [P, S, GB]), ALU.subtract))
                    elif piece == 12:
                        top.done(v.scalar_tensor_tensor(cand[:], an[:].rearrange("p s g -> p (s g)"), 0.0,
                                                        cand[:], ALU.is_gt, ALU.mult))
                    elif piece < 20:
                        r, replace = divmod(piece - 13, 2)
                        eight = c32[:, 8 * r:8 * r + 8]
                        if replace:
                            top.done(v.match_replace(out=cand[:], in_to_replace=eight, in_values=cand[:], imm_value=0.0))
                        else:
                            top.done(v.max(eight, cand[:]))
                    else:
                        v.tensor_scalar(idx[k % 2][:], c32[:, 0:S], -1.0, rowbase[:, 0:1], ALU.mult, ALU.add)\
                         .then_inc(idx_ok, 1)
                        if k == 0:
                            top.done(v.tensor_copy(degmin[:], c32[:, 0:1]))
                        else:
                            top.done(v.tensor_tensor(degmin[:], degmin[:], c32[:, 0:1], ALU.min))

                def take_max(k, g, half):
                    if half == 0:
                        for s in GROUPS[g]:
                            dve.wait_ge(g_in[s], (k + 1) * 16)
                    c = slice(half * P, (half + 1) * P)
                    v.tensor_reduce(part[:, g, c], gath[g][:, :, c].rearrange("p s c -> p c s"), AX_X, ALU.max)\
                     .then_inc(red_ok, 1)

                def whole_max(k):
                    dve.wait_ge(red_ok, (k + 1) * 2 * NR)
                    v.tensor_tensor(agg[:], part[:, 0, :], part[:, 1, :], ALU.max).then_inc(agg_ok, 1)

                def residual_norm(k, piece):
                    if piece == 0:
                        dve.wait_ge(lin_ok, k + 1)
                        wait_hx(dve, k)
                        v.scalar_tensor_tensor(x1[k % 4], kps[:, NG:2 * NG], 0.0, hx[k % 4][:, 1, :],
                                               ALU.max, ALU.add).then_inc(x1_ok, 1)
                    elif piece == 1:
                        dve.wait_ge(x1_ok, k + 1)
                        norm.done(v.bn_stats(st1[:], x1[k % 4]))
                    elif piece == 2:
                        norm.ready()
                        v.bn_aggr(mv1[:], st1[:]).then_inc(var1_ok, 1)
                    elif piece == 3:
                        dve.wait_ge(root1_ok, k + 1)
                        norm.done(v.reciprocal(rs1[:, 0:1], rs1[:, 0:1]))
                    else:
                        norm.ready()
                        v.scalar_tensor_tensor(rs1[:, 1:2], mv1[:, 0:1], -1.0, rs1[:, 0:1], ALU.mult, ALU.mult)\
                         .then_inc(ln1_ok, 1)

                def factors():
                    link(v.tensor_copy(sd2[:], sd[:]))
                    dve.sem_inc(sd_ok, 1)
                    s2, d2 = sd2[:, :, 0:H], sd2[:, :, H:2 * H]
                    v.tensor_scalar(kd[:], d2, BIG, None, ALU.mult)
                    link(v.tensor_scalar(negd[:], d2, -1.0, None, ALU.mult))
                    v.tensor_reduce(dmm[:, 0:H], d2.rearrange("p t h -> p h t"), AX_X, ALU.max)
                    v.tensor_reduce(dmm[:, H:2 * H], negd[:].rearrange("p t h -> p h t"), AX_X, ALU.max).then_inc(dd_ok, 1)
                    dve.wait_ge(dT_ps, 1)
                    link(v.tensor_reduce(drow[:], cps[0:2 * H, 0:P], AX_X, ALU.max))
                    v.tensor_scalar(ddiag[:], ident[0:2 * H, 0:2 * H], drow[:, 0:1], None, ALU.mult).then_inc(dd_ok, 1)
                    dve.wait_ge(db_ps, 1)
                    link(v.tensor_copy(dmax[:], cps[:, P:P + 2 * H]))
                    dmx = over(dmax[:, 0:H], 1, [P, NT, H])
                    v.tensor_tensor(tmpz[:], d2, dmx, ALU.subtract).then_inc(exp_in, 1)
                    link(v.tensor_tensor(tmpn[:], s2, dmx, ALU.add))
                    link(v.tensor_scalar(tmpp[:], tmpn[:], 0.0, None, ALU.max))
                    v.tensor_scalar(tmpn[:], tmpn[:], 0.0, None, ALU.min).then_inc(exp_in, 1)
                    link(v.tensor_reduce(gtmp[:, 0:1], dmax[:], AX_X, ALU.max))
                    link(v.tensor_scalar(gtmp[:, 0:1], gtmp[:, 0:1], 1.0e18, None, ALU.is_le))
                    link(v.tensor_tensor(good[:, 3:4], good[:, 3:4], gtmp[:, 0:1], ALU.min))
                    link(v.tensor_tensor(gtmp[:], dmax[:, 0:H], dmax[:, H:2 * H], ALU.add))
                    link(v.tensor_scalar(gtmp[:], gtmp[:], RANGE, None, ALU.is_le))
                    link(v.tensor_reduce(gtmp[:, 0:1], gtmp[:], AX_X, ALU.min))
                    link(v.tensor_tensor(good[:, 2:3], good[:, 2:3], gtmp[:, 0:1], ALU.min))
                    dve.wait_ge(exp_ok, 4)

                def values(g):
                    t = slice(2 * g, 2 * g + 2)
                    dve.wait_ge(hpl_in[g % 2], (g // 2 + 1) * 16)
                    free(dve, val_ok, g)
                    hv = hpl[g % 2].rearrange("p t (h e) -> p (t h) e", h=H)
                    for i, e in enumerate((eB, eB1)):
                        ee = e[:, t, :].rearrange("p t h -> p (t h)")
                        v.tensor_tensor(vf[:, :, i * (E + 1):i * (E + 1) + E], hv, over(ee, 2, [P, 2 * H, E]), ALU.mult)
                        ins = v.tensor_copy(vf[:, :, i * (E + 1) + E], ee)
                    link(ins)
                    o = val[:, 2 * g * H:(2 * g + 2) * H]
                    link(v.tensor_copy(o[:, :, 0, :], vf))
                    link(v.tensor_tensor(vf, vf, o[:, :, 0, :], ALU.subtract))
                    link(v.tensor_copy(o[:, :, 1, :], vf))
                    v.tensor_tensor(o[:, :, 2, :], vf, o[:, :, 1, :], ALU.subtract).then_inc(val_ok, 1)

                def unit_edges(n):
                    u, jt = divmod(n, NT)
                    q = u // H
                    if jt == 0:
                        dve.wait_ge(maskq_in[q % 2], (q // 2 + 1) * 16)
                    dve.wait_ge(relu_ok, n + 1)
                    free(dve, gt_used, n + 1 - D)
                    v.tensor_tensor(gt[n % D][:].rearrange("p (t r) -> p t r", t=Q),
                                    rb[n % D][:].rearrange("p (t r) -> p t r", t=Q),
                                    maskq[q % 2][:, :, jt, :], ALU.min).then_inc(gt_ok, 1)

                def each(ap, n=E):
                    return over(ap, 2, [P, Q, n])

                def unit_rows(u, piece):
                    q, h = u // H, u % H
                    t4 = slice(q * Q, (q + 1) * Q)
                    rows.ready()
                    if piece == 0:
                        dve.wait_ge(araw_ok, (u + 1) * Q)
                        rows.done(v.tensor_tensor(gs, gs, araw[:, :, 1, :], ALU.add))
                    elif piece == 1:
                        rows.done(v.tensor_tensor(gs, gs, araw[:, :, 2, :], ALU.add))
                    elif piece == 2:
                        dve.wait_ge(mraw_ok, 2 * (u + 1))
                        rows.done(v.tensor_tensor(ms, ms, mraw[:, :, 1, :], ALU.add))
                    elif piece == 3:
                        rows.done(v.tensor_tensor(ms, ms, mraw[:, :, 2, :], ALU.add))
                    elif piece == 4:
                        v.tensor_tensor(f0[:], ms, gs[:, :, E + 1:V], ALU.subtract).then_inc(mraw_used, 1)
                        rows.done(v.tensor_tensor(gs[:, :, 0:E + 1], gs[:, :, 0:E + 1], each(eA[:, t4, h], E + 1), ALU.mult))
                    elif piece == 5:
                        rows.done(v.tensor_tensor(f0[:], f0[:], each(eA1[:, t4, h], E + 1), ALU.mult))
                    elif piece == 6:
                        v.tensor_tensor(f0[:], f0[:], gs[:, :, 0:E + 1], ALU.add).then_inc(araw_used, 1)
                        dve.wait_ge(araw_used, u + 1)
                    elif piece == 7:
                        rows.done(v.tensor_scalar(rden[:], f0[:, :, E], 1.0e-37, None, ALU.max))
                    elif piece == 8:
                        rows.done(v.reciprocal(rden[:], rden[:]))
                    elif piece == 9:
                        rows.done(v.tensor_tensor(f1[:], f0[:, :, 0:E], each(rden[:]), ALU.mult))
                    elif piece == 10:
                        rows.done(v.tensor_tensor(f1[:], f1[:], over(bias_b[:, h, :], 1, [P, Q, E]), ALU.add))
                    elif piece == 11:
                        dve.wait_ge(hq_in, (q + 1) * 16)
                        v.scalar_tensor_tensor(f1[:], f1[:], 0.0, hq[:, :, h * E:(h + 1) * E], ALU.max, ALU.add)\
                         .then_inc(hq_used, 1)
                    elif piece == 12:
                        dve.wait_ge(msum_ok, (u + 1) * Q)
                        v.tensor_scalar(negm[:], msum[:], -1.0 / E, None, ALU.mult).then_inc(negm_ok, 1)
                    elif piece == 13:
                        dve.wait_ge(root2_ok, u + 1)
                        rows.done(v.reciprocal(var[:], var[:]))
                    elif piece == 14:
                        v.tensor_tensor(nm2[:], negm[:], var[:], ALU.mult).then_inc(nm2_ok, 1)
                    elif piece == 15:
                        dve.wait_ge(app_ok, (u + 1) * Q)
                        rows.done(v.tensor_tensor(f1[:], f1[:], over(gamma_b[:, h, :], 1, [P, Q, E]), ALU.mult))
                    elif piece == 16:
                        rows.done(v.tensor_tensor(f1[:], f1[:], over(beta_b[:, h, :], 1, [P, Q, E]), ALU.add))
                    else:
                        dve.wait_ge(xq_in, (q + 1) * 16)
                        o = outq[q % 2][:, :, h * E:(h + 1) * E]
                        v.tensor_tensor(o, f1[:], o, ALU.add).then_inc(unit_done, 1)

                TOP = {s: (2 * (s - 1), 2 * (s - 1) + 1) for s in range(1, 11)} | {11: (20, None)}
                ROWS_AT = {4: (0, 1), 5: (2, 3), 6: (4, 5), 7: (6, 7), 8: (8, 9), 9: (10, 11), 11: (12, None),
                           13: (13, None), 14: (14, None)}
                LATE = {0: 15, 1: 16, 2: 17}
                NORM = {7: (0,), 8: (1,), 9: (2,), 11: (3,), 12: (4,)}
                MAXES = {5: (0, 0), 6: (0, 1), 13: (1, 0), 14: (1, 1)}
                for j in range(STEPS):
                    if j == 0 and b2 is not None:
                        factors()
                    for s in range(NT):
                        ta, tb = TOP.get(s, (None, None))
                        ra, rb_ = ROWS_AT.get(s, (None, None))
                        if in_two(j - 1):
                            unit_edges((j - 1) * NT + s)
                        if s < 2 and in_one(j):
                            make_mask(j, s)
                        if in_one(j - 1) and ta is not None:
                            first_neighbours(j - 1, ta)
                        if in_two(j - 2) and ra is not None:
                            unit_rows(j - 2, ra)
                        if in_two(j - 3) and s in LATE:
                            unit_rows(j - 3, LATE[s])
                        for i in NORM.get(s, ()):
                            if in_one(j - 3):
                                residual_norm(j - 3, i)
                        if in_one(j - 1) and tb is not None:
                            first_neighbours(j - 1, tb)
                        if in_two(j - 2) and rb_ is not None:
                            unit_rows(j - 2, rb_)
                        if in_one(j - 2) and s in MAXES:
                            take_max(j - 2, *MAXES[s])
                        if in_one(j - 2) and s == 15:
                            whole_max(j - 2)
                        if j == 0 and b2 is not None and s % 2 == 1:
                            values(s // 2)
                    if j == NT and b1 is not None:
                        top.ready()
                        link(v.tensor_scalar(rowbase[:], rowbase[:], float(ROWS), None, ALU.add))
                        link(v.tensor_scalar(degmin[:], degmin[:], 0.0, None, ALU.is_gt))
                        link(v.tensor_tensor(good[:, 1:2], good[:, 1:2], degmin[:], ALU.min))
                        dve.wait_ge(chk_ok, 2 * NT)
                        link(v.tensor_reduce(gtmp[:, 0:1], chk[:], AX_X, ALU.max))
                        link(v.tensor_scalar(gtmp[:, 0:1], gtmp[:, 0:1], N / 8.0, None, ALU.is_le))
                        link(v.tensor_tensor(good[:, 0:1], good[:, 0:1], gtmp[:, 0:1], ALU.min))
            @block.tensor
            def _(pe):
                mm, turn = nc.tensor.matmul, nc.tensor.transpose

                def turn_activations(k):
                    pe.wait_ge(agg_ok, k + 1)
                    if k == 0 and both:
                        pe.wait_ge(exp_in, 1)
                    wait_hx(pe, k)
                    free(pe, hp_ok, 3 * k)
                    for i in range(2):
                        turn(cps[:, i * P:(i + 1) * P], hx[k % 4][:, 0, i * P:(i + 1) * P], ident[:])
                    for i in range(2):
                        ins = turn(cps[:, (2 + i) * P:(3 + i) * P], agg[:, i * P:(i + 1) * P], ident[:])
                    ins.then_inc(hT_ps, 1)

                def turn_mask(k, hf):
                    m = 2 * k + hf
                    pe.wait_ge(mask_ok, m + 1)
                    free(pe, mT_ok, m)
                    for i in range(NT // 2):
                        ins = turn(tps[:, i * P:(i + 1) * P], mask_h[hf][:, i * P:(i + 1) * P], identb[:])
                    ins.then_inc(turn_ok, 1)

                def dense0(k):
                    pe.wait_ge(hT_ok, k + 1)
                    free(pe, x1_ok, k)
                    free(pe, bytes_ok, min(k + 3, NT))
                    o = kps[:, NG:2 * NG]
                    for i in range(4):
                        mm(o, hT[:, i, :], w0_sb[:, i, :], start=(i == 0), stop=False)
                    mm(o, ones[0:1, :], b0_sb[:], start=False, stop=True).then_inc(lin_ok, 1)

                def group_bytes(k):
                    pe.wait_ge(mT_ok, 2 * k + 2)
                    free(pe, x1_ok, k - 2)
                    free(pe, bytes_ok, k)
                    for t in range(NT):
                        ins = mm(kps[:, t * GPT:(t + 1) * GPT], mT[k % 2][:, t, :], bits_w[:], start=True, stop=True)
                    ins.then_inc(keys_ok, 1)

                def turn_h1(k):
                    pe.wait_ge(h1_ok, k + 1)
                    for i in range(2):
                        ins = turn(cps[:, i * P:(i + 1) * P], h1[:, i * P:(i + 1) * P], ident[:])
                    ins.then_inc(h1T_ps, 1)

                def project1(k):
                    pe.wait_ge(h1T_ok, k + 1)
                    for i in range(2):
                        mm(cps[:, 0:W1N], h1T[:, i, :], r1[:, i, :], start=(i == 0), stop=(i == 1))
                    for i in range(2):
                        ins = mm(cps[0:H, 3 * P:4 * P], r1[:, i, C:C + H], h1T[:, i, :], start=(i == 0), stop=(i == 1))
                    ins.then_inc(hp_ps, 1)

                def factors():
                    pe.wait_ge(dd_ok, 1)
                    turn(cps[0:2 * H, 0:P], dmm[:], ident[:]).then_inc(dT_ps, 1)
                    pe.wait_ge(dd_ok, 2)
                    mm(cps[:, P:P + 2 * H], ones[0:2 * H, :], ddiag[:], start=True, stop=True).then_inc(db_ps, 1)

                def unit_edges(n):
                    u, jt = divmod(n, NT)
                    h = u % H
                    pe.wait_ge(gt_ok, n + 1)
                    for t in range(Q):
                        if jt == 0:
                            free(pe, araw_ok, (u - 1) * Q + t + 1)
                        ins = mm(acc[t][:, 0:K3 * V], gt[n % D][:, t * P:(t + 1) * P],
                                 val[:, jt * H + h].rearrange("p k v -> p (k v)"), start=(jt == 0), stop=(jt == NT - 1))
                    ins.then_inc(gt_used, 1)

                def unit_masked(u, pair, part_of):
                    q, h, w = u // H, u % H, K3 * (E + 1)
                    if part_of == 0:
                        pe.wait_ge(maskq_in[q % 2], (q // 2 + 1) * 16)
                        if u == 0 and pair == 0:
                            pe.wait_ge(val_ok, NT // 2)
                        free(pe, mraw_ok, 2 * u + pair)
                    i = part_of // 2
                    for jt in range(part_of % 2 * (NT // 2), (part_of % 2 + 1) * (NT // 2)):
                        ins = mm(macc[:, i * w:(i + 1) * w], maskq[q % 2][:, 2 * pair + i, jt, :],
                                 val[:, jt * H + h, :, E + 1:V], start=(jt == 0), stop=(jt == NT - 1))
                    if part_of == 3:
                        ins.then_inc(macc_ok, 1)

                for j in range(STEPS):
                    if j == 0 and b2 is not None:
                        factors()
                    for s in range(NT):
                        if s == 1 and in_one(j - 3):
                            turn_activations(j - 3)
                        if s == 2 and in_one(j):
                            turn_mask(j, 0)
                        if s == 5 and in_one(j - 3):
                            dense0(j - 3)
                        if s == 6 and in_one(j):
                            turn_mask(j, 1)
                        if s == 9 and in_one(j):
                            group_bytes(j)
                        if s == 13 and in_one(j - 3):
                            turn_h1(j - 3)
                        if s == 15 and in_one(j - 3):
                            project1(j - 3)
                        if in_two(j - 1) and 2 <= s < 6:
                            unit_masked(j - 1, 0, s - 2)
                        if in_two(j - 1) and 9 <= s < 13:
                            unit_masked(j - 1, 1, s - 9)
                        n = (j - 1) * NT + s - BEHIND
                        if b2 is not None and 0 <= n < NQ * H * NT:
                            unit_edges(n)

            @block.scalar
            def _(act):
                a = nc.scalar

                def activations_out(k):
                    act.wait_ge(hT_ps, k + 1)
                    a.copy(hT[:].rearrange("p i r -> p (i r)"), cps[:]).then_inc(hT_ok, 1)

                def check_entries(k, hf):
                    m = 2 * k + hf
                    act.wait_ge(adj_in[hf], (k + 1) * 16)
                    free(act, chk_ok, m)
                    a.activation(sq[:], adj_h[hf][:], ACT.Square, bias=mhalf[:, 0:1], accum_out=chk[:, m:m + 1])\
                     .then_inc(chk_ok, 1)

                def mask_out(b, k, hf):
                    m = 2 * k + hf
                    act.wait_ge(turn_ok, m + 1)
                    if hf == 0:
                        free(act, mT_out[k % 2], k // 2 * 16)
                    a.copy(mT[k % 2][:, hf * (NT // 2):(hf + 1) * (NT // 2), :].rearrange("p t r -> p (t r)"), tps[:])\
                     .then_inc(mT_ok, 1)
                    if hf == 1:
                        act.wait_ge(mT_ok, m + 1)
                        act.dma_start(maskT_d[b, k], mT[k % 2][:]).then_inc(mT_out[k % 2], 16)

                def root1(k):
                    act.wait_ge(var1_ok, k + 1)
                    a.activation(rs1[:, 0:1], mv1[:, 1:2], ACT.Sqrt, bias=epsc[:, 0:1]).then_inc(root1_ok, 1)

                def normalise(b, k):
                    act.wait_ge(ln1_ok, k + 1)
                    act.dma_start(x1_d[b, k], x1[k % 4]).then_inc(x1_out[k % 4], 16)
                    a.activation(h1[:], x1[k % 4], ACT.Relu, bias=rs1[:, 1:2], scale=rs1[:, 0:1]).then_inc(h1_ok, 1)

                def h1_out(k):
                    act.wait_ge(h1T_ps, k + 1)
                    a.copy(h1T[:].rearrange("p i r -> p (i r)"), cps[:, 0:2 * P]).then_inc(h1T_ok, 1)

                def projected_out(b, k):
                    act.wait_ge(hp_ps, k + 1)
                    free(act, hp_out[k % 2], k // 2 * 16)
                    free(act, e_out[k % 2], k // 2 * 16)
                    if k == 0 and both:
                        act.wait_ge(sd_ok, 1)
                    a.copy(hps[k % 2][:], cps[:, 0:C]).then_inc(hp_ok, 1)
                    a.copy(sd[:, k, :], cps[:, C:W1N]).then_inc(hp_ok, 1)
                    a.copy(eT[k % 2][:], cps[0:H, 3 * P:4 * P]).then_inc(hp_ok, 1)
                    act.wait_ge(hp_ok, 3 * (k + 1))
                    act.dma_start(hp_d[b, k], hps[k % 2][:]).then_inc(hp_out[k % 2], 16)
                    act.dma_start(src_d[b, :, k * P:(k + 1) * P], eT[k % 2][:]).then_inc(e_out[k % 2], 16)

                def factors():
                    act.wait_ge(exp_in, 1)
                    a.activation(eB[:], tmpz[:], ACT.Exp).then_inc(exp_ok, 1)
                    a.activation(eB1[:], tmpz[:], ACT.Exp, scale=SLOPE).then_inc(exp_ok, 1)
                    act.wait_ge(exp_in, 2)
                    a.activation(eA[:], tmpn[:], ACT.Exp, scale=1.0 - SLOPE).then_inc(exp_ok, 1)
                    a.activation(eA1[:], tmpp[:], ACT.Exp, scale=SLOPE - 1.0).then_inc(exp_ok, 1)

                def sums_out(u):
                    act.wait_ge(gt_used, (u + 1) * NT)
                    free(act, araw_used, u)
                    for t in range(Q):
                        a.copy(araw[:, t].rearrange("p k v -> p (k v)"), acc[t][:, 0:K3 * V]).then_inc(araw_ok, 1)

                def masked_out(u, pair):
                    act.wait_ge(macc_ok, 2 * u + pair + 1)
                    free(act, mraw_used, u)
                    a.copy(mraw[:, 2 * pair:2 * pair + 2].rearrange("p t k v -> p (t k v)"), macc[:, 0:2 * K3 * (E + 1)])\
                     .then_inc(mraw_ok, 1)

                def unit_signs(n):
                    u, jt = divmod(n, NT)
                    h = u % H
                    if jt == 0:
                        act.wait_ge(srcb_in[h % 2], (u // 2 + 1) * 16)
                    free(act, gt_ok, n + 1 - D)
                    a.activation(rb[n % D][:], srcb[h % 2][:], ACT.Relu, bias=kd[:, jt, h:h + 1], scale=BIG).then_inc(relu_ok, 1)

                def row_sums(u):
                    act.wait_ge(hq_used, u + 1)
                    for t in range(Q):
                        a.activation(f0[:, t, 0:E], f1[:, t, :], ACT.Identity, accum_out=msum[:, t:t + 1]).then_inc(msum_ok, 1)

                def row_squares(u):
                    act.wait_ge(negm_ok, u + 1)
                    for t in range(Q):
                        a.activation(f0[:, t, 0:E], f1[:, t, :], ACT.Square, bias=negm[:, t:t + 1],
                                     accum_out=var[:, t:t + 1]).then_inc(sq2_ok, 1)
                    act.wait_ge(sq2_ok, (u + 1) * Q)
                    a.activation(var[:], var[:], ACT.Sqrt, bias=epsc[:, 1:2], scale=1.0 / E).then_inc(root2_ok, 1)

                def row_scale(u):
                    act.wait_ge(nm2_ok, u + 1)
                    for t in range(Q):
                        a.activation(f1[:, t, :], f1[:, t, :], ACT.Identity, bias=nm2[:, t:t + 1],
                                     scale=var[:, t:t + 1]).then_inc(app_ok, 1)

                def store_out(b, q):
                    act.wait_ge(unit_done, (q + 1) * H)
                    act.dma_start(out[b, q * Q * P:(q + 1) * Q * P, :].rearrange("(t p) c -> p t c", p=P), outq[q % 2][:])\
                       .then_inc(out_st[q % 2], 16)

                for j in range(STEPS):
                    if j == 0 and b2 is not None:
                        factors()
                    for s in range(NT):
                        n = (j - 1) * NT + s + AHEAD
                        if b2 is not None and 0 <= n < NQ * H * NT:
                            unit_signs(n)
                        if s == 0 and in_one(j - 4):
                            projected_out(b1, j - 4)
                        if s == 2 and in_two(j - 2):
                            sums_out(j - 2)
                        if s < 2 and in_one(j):
                            check_entries(j, s)
                        if s == 3 and in_one(j - 3):
                            activations_out(j - 3)
                        if s == 4 and in_one(j):
                            mask_out(b1, j, 0)
                        if s == 8 and in_one(j):
                            mask_out(b1, j, 1)
                        if s == 7 and in_two(j - 1):
                            masked_out(j - 1, 0)
                        if s == 10 and in_one(j - 3):
                            root1(j - 3)
                        if s == 10 and in_two(j - 2):
                            row_sums(j - 2)
                        if s == 12 and in_two(j - 2):
                            row_squares(j - 2)
                        if s == 12 and in_one(j - 3):
                            normalise(b1, j - 3)
                        if s == 14 and in_one(j - 3):
                            h1_out(j - 3)
                        if s == 14 and in_two(j - 1):
                            masked_out(j - 1, 1)
                        if s == 15 and in_two(j - 2):
                            row_scale(j - 2)
                        if s == 4 and in_two(j - 3) and (j - 3) % H == H - 1:
                            store_out(b2, (j - 3) // H)
                if b1 is not None:
                    for s in mT_out + hp_out + e_out:
                        act.wait_ge(s, NT // 2 * 16)
                    for s in x1_out:
                        act.wait_ge(s, NT // 4 * 16)
                if b2 is not None:
                    for s in out_st:
                        act.wait_ge(s, NQ // 2 * 16)

        def direct_attention():
            adjg = sb("adjg", [P, N], I32)
            wgt = sb("wgt", [P, N])
            term = sb("term", [P, N])
            dstb = [sb(f"dstb{i}", [P, N]) for i in range(2)]
            hpg = sb("hpg", [P, NT, C])
            a_all = [sb(f"a_all{i}", [P, H, T, E]) for i in range(2)]
            prod = sb("prod", [P, H, T, E])
            sg = sb("sg", [P, NT, 2, H * T])
            dT = sb("dT", [H * T, N])
            pT = sb("pT", [P, N])
            sk = sb("sk", [P, H * T])
            hpk, xk, one = sb("hpk", [P, C]), sb("xk", [P, C]), sb("one", [P, E])
            mx, den, st, mv, root = (sb("mx", [P, 1]), sb("den", [P, 1]), sb("st", [P, 6]), sb("mv", [P, 2]),
                                     sb("root", [P, 1]))
            src_all = scratch("src_all", (NT, P, H * T))
            dst_all = scratch("dst_all", (H * T, N))
            gps = [ps(f"gps{i}", [P, 512]) for i in range(4)]
            ops = ps("ops", [P, 512])

            with nc.Fori(0, B) as b:
                with nc.Block() as block:
                    @block.sync
                    def _(sp):
                        sp.dma_start(hpg[:], hp_d[b].rearrange("t p c -> p t c")).then_inc(gen_in, 16)
                        for dst, a in zip(a_all, (a_src, a_dst)):
                            sp.dma_start(dst[:], a.partition_broadcast(P)).then_inc(gen_in, 16)
                        sp.wait_ge(sg_ok, NT)
                        sp.dma_start(src_all.rearrange("t p c -> p t c"), sg[:, :, 0, :]).then_inc(gen_out, 16)
                        sp.wait_ge(dT_ok, 4)
                        sp.dma_start(dst_all, dT[:]).then_inc(gen_out, 16)
                        sp.wait_ge(gen_out, 32)

                    @block.vector
                    def _(dve):
                        link = Chain(dve, dve_c, fresh=True).link
                        dve.wait_ge(gen_in, 48)
                        for t in range(NT):
                            for i in range(2):
                                hv = hpg[:, t, :].rearrange("p (h e) -> p h e", h=H)
                                for y in range(T):
                                    ins = nc.vector.tensor_tensor(prod[:, :, y, :], hv, a_all[i][:, :, y, :], ALU.mult)
                                link(ins)
                                link(nc.vector.tensor_reduce(sg[:, t, i, :], prod[:].rearrange("p h y e -> p (h y) e"),
                                                             AX_X, ALU.add))
                            dve.sem_inc(sg_ok, 1)

                    @block.tensor
                    def _(pe):
                        for t in range(NT):
                            pe.wait_ge(sg_ok, t + 1)
                            nc.tensor.transpose(gps[t // 4][0:H * T, t % 4 * P:(t % 4 + 1) * P], sg[:, t, 1, :], ident[:])\
                              .then_inc(dT_t, 1)

                    @block.scalar
                    def _(act):
                        for g in range(4):
                            act.wait_ge(dT_t, 4 * (g + 1))
                            nc.scalar.copy(dT[:, g * 4 * P:(g + 1) * 4 * P], gps[g][0:H * T, :]).then_inc(dT_ok, 1)
                reset()

                with nc.Fori(0, NT) as k:
                    with nc.Block() as block:
                        @block.sync
                        def _(sp):
                            for dst, src in ((adjg[:], adj.rearrange("b (k p) j -> b k p j", p=P)[b, k]), (sk[:], src_all[k]), (hpk[:], hp_d[b, k]),
                                             (xk[:], x1_d[b, k])):
                                sp.dma_start(dst, src).then_inc(row_in, 16)
                            for n in range(H * T):
                                free(sp, dst_used, n - 1)
                                sp.dma_start(dstb[n % 2][:], dst_all[n].partition_broadcast(P)).then_inc(dst_in[n % 2], 16)
                            sp.wait_ge(head_ok, H)
                            sp.dma_start(out.rearrange("b (k p) c -> b k p c", p=P)[b, k], xk[:]).then_inc(gen_out, 16)
                            sp.wait_ge(gen_out, 16)

                        @block.vector
                        def _(dve):
                            v = nc.vector
                            link = Chain(dve, dve_c, fresh=True).link
                            dve.wait_ge(row_in, 64)
                            for h in range(H):
                                free(dve, pT_ps, 4 * h)
                                for t in range(T):
                                    n = h * T + t
                                    dve.wait_ge(dst_in[n % 2], (n // 2 + 1) * 16)
                                    v.tensor_scalar(term[:], dstb[n % 2][:], sk[:, n:n + 1], None, ALU.add).then_inc(dst_used, 1)
                                    dve.wait_ge(dst_used, n + 1)
                                    link(v.scalar_tensor_tensor(term[:] if t else wgt[:], adjg[:], float(t + 1), term[:],
                                                                ALU.is_equal, ALU.mult))
                                    if t:
                                        link(v.tensor_tensor(wgt[:], wgt[:], term[:], ALU.add))
                                link(v.scalar_tensor_tensor(wgt[:], wgt[:], SLOPE, wgt[:], ALU.mult, ALU.max))
                                link(v.tensor_scalar(term[:], adjg[:], 0.0, NEG, ALU.is_equal, ALU.mult))
                                link(v.tensor_tensor(wgt[:], wgt[:], term[:], ALU.add))
                                link(v.tensor_reduce(mx[:], wgt[:], AX_X, ALU.max))
                                v.tensor_scalar(mx[:], mx[:], -1.0, None, ALU.mult).then_inc(w_ok, 1)
                                dve.wait_ge(p_ok, h + 1)
                                dve.wait_ge(o_ps, h + 1)
                                link(v.reciprocal(den[:], den[:]))
                                link(v.tensor_scalar(one[:], ops[:, 0:E], den[:, 0:1], None, ALU.mult))
                                link(v.tensor_tensor(one[:], one[:], bias_b[:, h, :], ALU.add))
                                link(v.scalar_tensor_tensor(one[:], one[:], 0.0, hpk[:, h * E:(h + 1) * E], ALU.max, ALU.add))
                                link(v.bn_stats(st[:], one[:]))
                                link(v.bn_aggr(mv[:], st[:]))
                                dve.sem_inc(mv_ok, 1)
                                dve.wait_ge(root_ok, h + 1)
                                link(v.reciprocal(root[:], root[:]))
                                link(v.tensor_scalar(one[:], one[:], mv[:, 0:1], root[:, 0:1], ALU.subtract, ALU.mult))
                                link(v.tensor_tensor(one[:], one[:], gamma_b[:, h, :], ALU.mult))
                                link(v.tensor_tensor(one[:], one[:], beta_b[:, h, :], ALU.add))
                                xh = xk[:, h * E:(h + 1) * E]
                                v.tensor_tensor(xh, xh, one[:], ALU.add).then_inc(head_ok, 1)
                                dve.wait_ge(head_ok, h + 1)

                        @block.scalar
                        def _(act):
                            for h in range(H):
                                act.wait_ge(w_ok, h + 1)
                                nc.scalar.activation(wgt[:], wgt[:], ACT.Exp, bias=mx[:, 0:1], accum_out=den[:, 0:1])\
                                  .then_inc(p_ok, 1)
                                for g in range(4):
                                    act.wait_ge(pT_ps, 4 * h + g + 1)
                                    free(act, o_ps, h)
                                    nc.scalar.copy(pT[:, g * 4 * P:(g + 1) * 4 * P], gps[g][:]).then_inc(pT_ok, 1)
                                act.wait_ge(mv_ok, h + 1)
                                nc.scalar.activation(root[:], mv[:, 1:2], ACT.Sqrt, bias=epsc[:, 1:2]).then_inc(root_ok, 1)

                        @block.tensor
                        def _(pe):
                            for h in range(H):
                                pe.wait_ge(p_ok, h + 1)
                                for g in range(4):
                                    free(pe, pT_ok, 4 * (h - 1) + g + 1)
                                    for t in range(4 * g, 4 * g + 4):
                                        ins = nc.tensor.transpose(gps[g][:, t % 4 * P:(t % 4 + 1) * P],
                                                                  wgt[:, t * P:(t + 1) * P], ident[:])
                                    ins.then_inc(pT_ps, 1)
                                pe.wait_ge(pT_ok, 4 * (h + 1))
                                for t in range(NT):
                                    ins = nc.tensor.matmul(ops[:, 0:E], pT[:, t * P:(t + 1) * P],
                                                           hpg[:, t, h * E:(h + 1) * E], start=(t == 0), stop=(t == NT - 1))
                                ins.then_inc(o_ps, 1)
                    reset()

        with ExitStack() as turns:
            turn_of_engines(0, None)
        reset()
        with nc.Fori(0, B - 1) as b:
            with ExitStack() as turns:
                turn_of_engines(b + 1, b)
            reset()
        with ExitStack() as turns:
            turn_of_engines(None, B - 1)

        reset()
        with nc.Block() as block:
            @block.tensor
            def _(pe):
                nc.tensor.matmul(cps[0:1, 0:4], ones[:, 0:1], good[:], start=True, stop=True).then_inc(good_ps, 1)

            @block.vector
            def _(dve):
                dve.wait_ge(good_ps, 1)
                nc.vector.tensor_reduce(gsum[:], cps[0:1, 0:4], AX_X, ALU.add).then_inc(good_ok, 1)
                dve.wait_ge(good_ok, 1)
                nc.vector.tensor_copy(gsum_i[:], gsum[:]).then_inc(good_ok, 1)
                dve.wait_ge(good_ok, 2)
        reset()
        fast.close()
        all_good = nc.values_load(gsum_i[0:1, 0:1], min_val=0, max_val=4 * P)
        with nc.If(all_good < 4 * P):
            direct_attention()
            nc.all_engine_barrier()
        nc.end_all_ifs()


def constants():
    i = np.arange(P)
    bits = np.where(i[:, None] // GB == np.arange(GPT)[None, :], 1 << (i[:, None] % GB), 0)
    g = np.arange(NG)
    b = np.broadcast_to(np.arange(GB), (P, GB))
    return {
        "c_ident": np.eye(P, dtype=np.float32),
        "c_bits": bits.astype(mybir.dt.np(BF16)),
        "c_base": np.broadcast_to((256 * (NG - g)).astype(np.float32), (P, NG)).copy(),
        "c_bit": (1 << b).astype(np.int32),
        "c_ofs": b.astype(np.int32),
    }


_INS = ["x", "adj", "L0_gnn_W", "L0_gnn_b", "L1_gnn_W", "L1_gnn_a_src", "L1_gnn_a_dst", "L1_gnn_bias",
        "L1_gnn_ln_gamma", "L1_gnn_ln_beta"]


def kernel(**inputs):
    import concourse.bacc as bacc
    from concourse.bass_utils import run_bass_kernel_spmd

    nc = bacc.Bacc("TRN2", target_bir_lowering=False, num_devices=1)
    arrays, args = {}, []
    for name, a in [(n, inputs[n]) for n in _INS] + list(constants().items()):
        a = np.ascontiguousarray(a)
        arrays[name] = a
        args.append(nc.dram_tensor(name, a.shape, mybir.dt.from_np(a.dtype), kind="ExternalInput").ap())
    args.append(nc.dram_tensor("out", (B, N, C), F32, kind="ExternalOutput").ap())
    graph_layers(nc, *args)
    r = run_bass_kernel_spmd(nc, [arrays], core_ids=[0])
    return r.results[0]["out"]
```

```python
from contextlib import ExitStack

import numpy as np

import concourse.bass as bass
from concourse import mybir

ALU = mybir.AluOpType
ACT = mybir.ActivationFunctionType
AX_X = mybir.AxisListType.X
F32 = mybir.dt.float32
BF16 = mybir.dt.bfloat16
I32 = mybir.dt.int32
U32 = mybir.dt.uint32

P = 128
B, N, C = 8, 2048, 256
S = 25
H, E = 4, 64
T = 5
NT = N // P
EPS0 = 1e-5
EPS1 = 1e-6
NEG = -1.0e9
SLOPE = 0.01
ROWS = N + 1
GB = 8
NG = N // GB
GPT = P // GB
GROUPS = (range(0, 12), range(12, S))
NR = len(GROUPS)
V = 2 * E + 2
K3 = 3
BIG = 2.0 ** 64
RANGE = 60.0
Q = 4
NQ = NT // Q
D = 7
AHEAD, BEHIND = 3, 2


class Chain:

    count = {}

    def __init__(self, eng, sem, fresh=False):
        self.eng, self.sem, self.last = eng, sem, 0
        if fresh:
            Chain.count[sem.num] = 0

    def done(self, ins):
        Chain.count[self.sem.num] += 1
        self.last = Chain.count[self.sem.num]
        ins.then_inc(self.sem, 1)

    def ready(self):
        free(self.eng, self.sem, self.last)

    def link(self, ins):
        self.done(ins)
        self.ready()


def free(eng, sem, n):
    if n > 0:
        eng.wait_ge(sem, n)


def over(ap, axis, shape):
    return ap.unsqueeze(axis).to_broadcast(shape)


def graph_layers(nc, x, adj, w0, b0, w1, a_src, a_dst, bias1, gamma1, beta1, c_ident, c_bits, c_base, c_bit, c_ofs, out):
    with ExitStack() as ctx:
        fast = ExitStack()
        owner = [ctx]

        def sb(name, shape, dt=F32):
            return owner[-1].enter_context(nc.sbuf_tensor(name, shape, dt))

        def ps(name, shape, dt=F32):
            return owner[-1].enter_context(nc.psum_tensor(name, shape, dt))

        sems = []

        def sem(name):
            sems.append(ctx.enter_context(nc.semaphore(name)))
            return sems[-1]

        def reset():
            ids = sorted(s.num for s in sems)
            assert ids == list(range(ids[0], ids[-1] + 1))
            nc.gpsimd.dma_reset(range(ids[0], ids[-1] + 1))
            nc.gpsimd.sem_clear(range(ids[0], ids[-1] + 1))
            nc.all_engine_barrier()

        def scratch(name, shape, dt=F32):
            return nc.dram_tensor(name, shape, dt, kind="Internal").ap()

        table = scratch("table", (B * ROWS, C))
        maskT_d = scratch("maskT_d", (B, NT, P, NT, P), BF16)
        x1_d = scratch("x1_d", (B, NT, P, C))
        hp_d = scratch("hp_d", (B, NT, P, C))
        src_d = scratch("src_d", (B, H, N))
        table_g = table.rearrange("(b r) c -> b r c", b=B)

        ident = sb("ident", [P, P])
        identb = sb("identb", [P, P], BF16)
        good = sb("good", [P, 3])
        gsum, gsum_i = sb("gsum", [1, 2]), sb("gsum_i", [1, 1], I32)
        odd = sb("odd", [P, 1])
        bits_w = sb("bits_w", [P, GPT], BF16)
        base = sb("base", [P, NG])
        bitc = sb("bitc", [P, GB], I32)
        ofsc = sb("ofsc", [P, GB], I32)
        ones = sb("ones", [P, P])
        w0_sb = sb("w0_sb", [P, 4, C])
        b0_sb = sb("b0_sb", [1, C])
        r1 = sb("r1", [P, 2, C + 2 * H])
        bias_b = sb("bias_b", [P, H, E])
        gamma_b = sb("gamma_b", [P, H, E])
        beta_b = sb("beta_b", [P, H, E])
        zero_b = sb("zero_b", [B, C])
        minus1 = sb("minus1", [P, 1])
        epsc = sb("epsc", [P, 2])

        owner.append(fast)
        x0 = [sb(f"x0_{i}", [P, Q, C]) for i in range(2)]
        st0 = sb("st0", [P, Q, 6])
        mv0 = sb("mv0", [P, Q, 2])
        rs0 = [sb(f"rs0_{i}", [P, Q]) for i in range(2)]
        nm0 = [sb(f"nm0_{i}", [P, Q]) for i in range(2)]

        adj_h = [sb(f"adj_h{i}", [P, N // 2], I32) for i in range(2)]
        mask_h = [sb(f"mask_h{i}", [P, N // 2], BF16) for i in range(2)]
        gtmp = sb("gtmp", [P, H])
        degmin = sb("degmin", [P, 1])
        chk = sb("chk", [P, 2, 2 * NT])
        mT = [sb(f"mT{i}", [P, NT, P], BF16) for i in range(2)]
        key = sb("key", [P, NG])
        k32 = sb("k32", [P, 32])
        ki = sb("ki", [P, S], I32)
        b8 = sb("b8", [P, S], I32)
        an = sb("an", [P, S, GB], I32)
        cand = sb("cand", [P, S * GB])
        c32 = sb("c32", [P, 32])
        rowbase = sb("rowbase", [P, 1])
        idx = [sb(f"idx{i}", [P, S], U32) for i in range(2)]
        gath = [sb(f"gath{g}", [P, len(GROUPS[g]), C]) for g in range(NR)]
        part = sb("part", [P, NR, C])
        hx = [sb(f"hx{i}", [P, 2, C]) for i in range(4)]
        agg = sb("agg", [P, C])
        hT = sb("hT", [P, 4, P])
        x1 = [hx[i][:, 1, :] for i in range(4)]
        st1 = sb("st1", [P, 6])
        mv1 = sb("mv1", [P, 2])
        rs1 = sb("rs1", [P, 2])
        h1 = sb("h1", [P, C])
        h1T = sb("h1T", [P, 2, P])
        hps = [sb(f"hps{i}", [P, C]) for i in range(2)]
        sd = sb("sd", [P, NT, 2 * H])
        eT = [sb(f"eT{i}", [H, P]) for i in range(2)]

        sd2 = sb("sd2", [P, NT, 2 * H])
        dmm = sb("dmm", [P, 2 * H])
        drow = sb("drow", [2 * H, 1])
        ddiag = sb("ddiag", [2 * H, 2 * H])
        dmax = sb("dmax", [P, 2 * H])
        tmpz = sb("tmpz", [P, NT, H])
        tmpn = sb("tmpn", [P, NT, H])
        tmpp = sb("tmpp", [P, NT, H])
        negd = sb("negd", [P, NT, H])
        eB = sb("eB", [P, NT, H])
        eB1 = sb("eB1", [P, NT, H])
        eA = sb("eA", [P, NT, H])
        eA1 = sb("eA1", [P, NT, H])
        flat = sb("flat", [P, Q * K3 * V])
        vf = [flat[:, i * H * V:(i + 1) * H * V].rearrange("p (a v) -> p a v", v=V) for i in range(3)]
        araw = flat[:].rearrange("p (t k v) -> p t k v", t=Q, k=K3)
        mraw = sb("mraw", [P, Q, K3, E + 1])
        kd = sb("kd", [P, NT, H])
        asrc, adst, wa_tmp = (flat[:, i * C:(i + 1) * C].rearrange("p (h e) -> p h e", h=H) for i in range(3))
        val = sb("val", [P, NT * H, K3, V], BF16)
        maskq = [sb(f"maskq{i}", [P, Q, NT, P], BF16) for i in range(2)]
        srcb = [sb(f"srcb{i}", [P, Q * P]) for i in range(2)]
        gt = [sb(f"gt{i}", [P, Q * P], BF16) for i in range(D)]
        rb = [sb(f"rb{i}", [P, Q * P], BF16) for i in range(D)]
        hq = sb("hq", [P, Q, C])
        hpl = [hq[:, 2 * i:2 * i + 2, :] for i in range(2)]
        gs, ms = araw[:, :, 0, :], mraw[:, :, 0, :]
        f0 = sb("f0", [P, Q, E + 1])
        f1 = sb("f1", [P, Q, E])
        rden = sb("rden", [P, Q])
        msum = sb("msum", [P, Q])
        negm = sb("negm", [P, Q])
        var = sb("var", [P, Q])
        nm2 = sb("nm2", [P, Q])
        outq = x0

        acc = [ps(f"acc{i}", [P, 512]) for i in range(Q)]
        macc = ps("macc", [P, 512])
        tps = ps("tps", [P, 1024], BF16)
        kps = ps("kps", [P, 512])
        cps = ps("cps", [P, 512])

        owner.pop()

        const_in, const_ok = sem("const_in"), sem("const_ok")
        r1_ok = sem("r1_ok")
        dve_c = sem("dve_c")
        x0_in = [sem(f"x0_in{i}") for i in range(2)]
        x0_var, x0_root, x0_norm, x0_relu = sem("x0_var"), sem("x0_root"), sem("x0_norm"), sem("x0_relu")
        var1_ok, root1_ok, root2_ok = sem("var1_ok"), sem("root1_ok"), sem("root2_ok")
        x0_out = [sem(f"x0_out{i}") for i in range(2)]
        zero_out = sem("zero_out")
        adj_in = [sem(f"adj_in{i}") for i in range(2)]
        hx_in = [sem(f"hx_in{i}") for i in range(4)]
        mask_ok = sem("mask_ok")
        turn_ok, mT_ok, keys_ok, idx_ok = sem("turn_ok"), sem("mT_ok"), sem("keys_ok"), sem("idx_ok")
        g_in = [sem(f"g_in{s}") for s in range(S)]
        red_ok, agg_ok = sem("red_ok"), sem("agg_ok")
        hT_ps, hT_ok, lin_ok, x1_ok, ln1_ok, h1_ok = (sem("hT_ps"), sem("hT_ok"), sem("lin_ok"), sem("x1_ok"),
                                                      sem("ln1_ok"), sem("h1_ok"))
        h1T_ps, h1T_ok, hp_ps, hp_ok = sem("h1T_ps"), sem("h1T_ok"), sem("hp_ps"), sem("hp_ok")
        mT_out = [sem(f"mT_out{i}") for i in range(2)]
        x1_out = [sem(f"x1_out{i}") for i in range(4)]
        hp_out = [sem(f"hp_out{i}") for i in range(2)]
        e_out = [sem(f"e_out{i}") for i in range(2)]
        sd_ok = sem("sd_ok")
        dT_ps, dd_ok, db_ps, exp_in, exp_ok = sem("dT_ps"), sem("dd_ok"), sem("db_ps"), sem("exp_in"), sem("exp_ok")
        hpl_in = [sem(f"hpl_in{i}") for i in range(2)]
        whole_ok, first_ok, rest_ok, second_ok, val_ok = (sem("whole_ok"), sem("first_ok"), sem("rest_ok"),
                                                          sem("second_ok"), sem("val_ok"))
        maskq_in = [sem(f"maskq_in{i}") for i in range(2)]
        srcb_in = [sem(f"srcb_in{i}") for i in range(2)]
        hq_in, xq_in, relu_ok, hq_used = sem("hq_in"), sem("xq_in"), sem("relu_ok"), sem("hq_used")
        bytes_ok, araw_ok, araw_used, mraw_ok, mraw_used = (sem("bytes_ok"), sem("araw_ok"), sem("araw_used"),
                                                            sem("mraw_ok"), sem("mraw_used"))
        msum_ok, negm_ok, sq2_ok, nm2_ok, app_ok = (sem("msum_ok"), sem("negm_ok"), sem("sq2_ok"),
                                                           sem("nm2_ok"), sem("app_ok"))
        gt_ok, gt_used = sem("gt_ok"), sem("gt_used")
        macc_ok = sem("macc_ok")
        unit_done = sem("unit_done")
        out_st = [sem(f"out_st{i}") for i in range(2)]

        good_ps, gen_in, gen_out, sg_ok, dT_t, dT_ok = (sem("good_ps"), sem("gen_in"), sem("gen_out"),
                                                                 sem("sg_ok"), sem("dT_t"), sem("dT_ok"))
        row_in, dst_in, dst_used, w_ok, p_ok = (sem("row_in"), [sem(f"dst_in{i}") for i in range(2)], sem("dst_used"),
                                                sem("w_ok"), sem("p_ok"))
        pT_ps, pT_ok, o_ps, mv_ok, root_ok, head_ok = (sem("pT_ps"), sem("pT_ok"), sem("o_ps"), sem("mv_ok"),
                                                       sem("root_ok"), sem("head_ok"))

        W1N = C + 2 * H
        STEPS = range(-1, NT + 3)

        with nc.Block() as block:
            @block.sync
            def _(sp):
                def row_bc(a, n):
                    return a.rearrange("h e -> (h e)").partition_broadcast(n)

                for dst, src in ((ident[:], c_ident), (base[:], c_base), (bitc[:], c_bit), (ofsc[:], c_ofs),
                                 (bits_w[:], c_bits), (w0_sb[:], w0.rearrange("(k p) o -> p k o", p=P)),
                                 (b0_sb[:], b0.unsqueeze(0)),
                                 (bias_b[:].rearrange("p h e -> p (h e)"), row_bc(bias1, P)),
                                 (gamma_b[:].rearrange("p h e -> p (h e)"), row_bc(gamma1, P)),
                                 (beta_b[:].rearrange("p h e -> p (h e)"), row_bc(beta1, P)),
                                 (asrc, a_src[:, 0, :].partition_broadcast(P)),
                                 (adst, a_dst[:, 0, :].partition_broadcast(P))):
                    sp.dma_start(dst, src).then_inc(const_in, 16)
                for k in range(2):
                    sp.dma_start(r1[:, k, 0:C].rearrange("p (h e) -> p h e", h=H),
                                 w1[:, k * P:(k + 1) * P, :].rearrange("h p e -> p h e")).then_inc(const_in, 16)
                sp.wait_ge(const_ok, 2)
                sp.dma_start(table_g[:, N, :], zero_b[:]).then_inc(zero_out, 16)


                sp.wait_ge(zero_out, 16)

            @block.vector
            def _(dve):
                v = nc.vector
                link = Chain(dve, dve_c, fresh=True).link
                v.memset(ones[:], 1.0).then_inc(const_ok, 1)
                link(v.memset(rowbase[:], float(N)))
                v.memset(zero_b[:], 0.0).then_inc(const_ok, 1)
                v.memset(minus1[:], -1.0)
                v.memset(odd[:], 0.0)
                v.memset(good[:], 1.0)
                v.memset(epsc[:, 0:1], EPS0)
                v.memset(epsc[:, 1:2], EPS1).then_inc(const_ok, 1)
                dve.wait_ge(const_in, 16 * 14)
                v.tensor_copy(identb[:], ident[:]).then_inc(const_ok, 1)
                for k in range(2):
                    w = r1[:, k, 0:C].rearrange("p (h e) -> p h e", h=H)
                    for j, a in enumerate((asrc, adst)):
                        link(v.tensor_tensor(wa_tmp, w, a, ALU.mult))
                        link(v.tensor_reduce(r1[:, k, C + H * j:C + H * j + H], wa_tmp, AX_X, ALU.add))
                dve.sem_inc(r1_ok, 1)


        reset()

        with nc.Block() as block:
            @block.sync
            def _(sp):
                for q in range(NQ):
                    free(sp, x0_out[q % 2], q // 2 * 16)
                    sp.dma_start(x0[q % 2][:], x[0, q * Q * P:(q + 1) * Q * P, :].rearrange("(t p) c -> p t c", p=P))\
                      .then_inc(x0_in[q % 2], 16)

            @block.vector
            def _(dve):
                v = nc.vector
                link = Chain(dve, dve_c, fresh=True).link
                for q in range(NQ):
                    dve.wait_ge(x0_in[q % 2], (q // 2 + 1) * 16)
                    for t in range(Q):
                        ins = v.bn_stats(st0[:, t, :], x0[q % 2][:, t, :])
                    link(ins)
                    for t in range(Q):
                        ins = v.bn_aggr(mv0[:, t, :], st0[:, t, :])
                    link(ins)
                    ins = v.tensor_copy(rs0[q % 2][:], mv0[:, :, 1])
                    ins.then_inc(x0_var, 1)
                    dve.wait_ge(x0_root, q + 1)
                    link(v.reciprocal(rs0[q % 2][:], rs0[q % 2][:]))
                    v.scalar_tensor_tensor(nm0[q % 2][:], mv0[:, :, 0], -1.0, rs0[q % 2][:], ALU.mult, ALU.mult)\
                     .then_inc(x0_norm, 1)

            @block.scalar
            def _(act):
                for q in range(NQ):
                    act.wait_ge(x0_var, q + 1)
                    nc.scalar.activation(rs0[q % 2][:], rs0[q % 2][:], ACT.Sqrt, bias=epsc[:, 0:1]).then_inc(x0_root, 1)
                    act.wait_ge(x0_norm, q + 1)
                    for t in range(Q):
                        nc.scalar.activation(x0[q % 2][:, t, :], x0[q % 2][:, t, :], ACT.Relu,
                                             bias=nm0[q % 2][:, t:t + 1], scale=rs0[q % 2][:, t:t + 1])\
                          .then_inc(x0_relu, 1)
                    act.wait_ge(x0_relu, (q + 1) * Q)
                    act.dma_start(table_g[0, q * Q * P:(q + 1) * Q * P, :].rearrange("(t p) c -> p t c", p=P),
                                  x0[q % 2][:]).then_inc(x0_out[q % 2], 16)
                for i in range(2):
                    act.wait_ge(x0_out[i], NQ // 2 * 16)
        reset()

        def wait_hx(eng, k):
            eng.wait_ge(hx_in[k % 4], (k // 4 + 1) * 32)

        def table_quarter(j, s, offset):
            c, rest = divmod(j * NT + s - offset, NT // 2)
            return c if rest == 0 and 0 <= c < (B - 1) * NQ else None

        def turn_of_engines(b1, b2):
            last = b1 is None
            both = b1 is not None and b2 is not None
            first = b2 is None
            block = turns.enter_context(nc.Block())

            def in_one(k):
                return b1 is not None and 0 <= k < NT

            def in_two(u):
                return b2 is not None and 0 <= u < NQ * H

            @block.sync
            def _(sp):
                def load_adj(b, k, hf):
                    free(sp, mask_ok, 2 * k + hf - 1)
                    sp.dma_start(adj_h[hf][:], adj[b, k * P:(k + 1) * P, hf * (N // 2):(hf + 1) * (N // 2)])\
                      .then_inc(adj_in[hf], 16)

                def load_hx(b, k):
                    free(sp, x1_out[k % 4], k // 4 * 16)
                    free(sp, h1_ok, k - 3)
                    sp.dma_start(hx[k % 4][:, 0, :], table_g[b, k * P:(k + 1) * P, :]).then_inc(hx_in[k % 4], 16)
                    sp.dma_start(hx[k % 4][:, 1, :], x[b, k * P:(k + 1) * P, :]).then_inc(hx_in[k % 4], 16)

                def store_mask(b, k):
                    sp.wait_ge(mT_ok, 2 * k + 2)
                    sp.dma_start(maskT_d[b, k], mT[k % 2][:]).then_inc(mT_out[k % 2], 16)

                def store_x1(b, k):
                    sp.wait_ge(x1_ok, k + 1)
                    sp.dma_start(x1_d[b, k], x1[k % 4]).then_inc(x1_out[k % 4], 16)

                def store_projected(b, k):
                    sp.wait_ge(hp_ok, 3 * (k + 1))
                    sp.dma_start(hp_d[b, k], hps[k % 2][:]).then_inc(hp_out[k % 2], 16)
                    sp.dma_start(src_d[b, :, k * P:(k + 1) * P], eT[k % 2][:]).then_inc(e_out[k % 2], 16)

                def load_values(b, g):
                    free(sp, whole_ok, 2 * (g - 1))
                    sp.dma_start(hpl[g % 2], hp_d[b, 2 * g:2 * g + 2].rearrange("t p c -> p t c"))\
                      .then_inc(hpl_in[g % 2], 16)

                def load_mask(b, q, t):
                    free(sp, gt_used, (q - 1) * H * NT)
                    sp.dma_start(maskq[q % 2][:, t], maskT_d[b, q * Q + t]).then_inc(maskq_in[q % 2], 16)

                def load_src(b, u):
                    q, h = u // H, u % H
                    free(sp, relu_ok, (u - 1) * NT)
                    sp.dma_start(srcb[h % 2][:], src_d[b, h, q * Q * P:(q + 1) * Q * P].partition_broadcast(P))\
                      .then_inc(srcb_in[h % 2], 16)

                def load_x1(b, q):
                    free(sp, out_st[q % 2], q // 2 * 16)
                    sp.dma_start(outq[q % 2][:], x1_d[b, q * Q:(q + 1) * Q].rearrange("t p c -> p t c")).then_inc(xq_in, 16)

                def load_projected(b, q):
                    sp.wait_ge(whole_ok, NT)
                    free(sp, hq_used, q * H)
                    sp.dma_start(hq[:], hp_d[b, q * Q:(q + 1) * Q].rearrange("t p c -> p t c")).then_inc(hq_in, 16)

                def store_out(b, q):
                    sp.wait_ge(unit_done, (q + 1) * H)
                    sp.dma_start(out[b, q * Q * P:(q + 1) * Q * P, :].rearrange("(t p) c -> p t c", p=P), outq[q % 2][:])\
                      .then_inc(out_st[q % 2], 16)

                def rows_of(ap, c):
                    g, q = divmod(c, NQ)
                    return ap[1 + g, q * Q * P:(q + 1) * Q * P, :].rearrange("(t p) c -> p t c", p=P)

                def load_x0(c):
                    free(sp, x0_out[c % 2], c // 2 * 16)
                    sp.dma_start(x0[c % 2][:], rows_of(x, c)).then_inc(x0_in[c % 2], 16)

                def store_table(c):
                    sp.wait_ge(x0_relu, (c + 1) * Q)
                    sp.dma_start(rows_of(table_g, c), x0[c % 2][:]).then_inc(x0_out[c % 2], 16)

                if b2 is not None:
                    load_values(b2, 0)
                    load_values(b2, 1)
                if b1 is not None:
                    for hf in range(2):
                        load_adj(b1, 0, hf)
                    load_hx(b1, 0)
                for j in STEPS:
                    i = j + 1
                    for s in range(NT):
                        if first:
                            for offset, piece in ((0, load_x0), (8, store_table)):
                                c = table_quarter(j, s, offset)
                                if c is not None:
                                    piece(c)
                        if s == 0 and in_one(i - 4):
                            store_projected(b1, i - 4)
                        if j == 0 and b2 is not None and s % 2 == 0 and 2 <= s // 2 + 2 < NT // 2:
                            load_values(b2, s // 2 + 2)
                        if s % 4 == 1 and j == 0 and b2 is not None:
                            load_mask(b2, 0, s // 4)
                        if s == 1 and in_two(j):
                            load_src(b2, j)
                        if s == 2 and in_two(j - 1) and (j - 1) % H == 0:
                            load_x1(b2, (j - 1) // H)
                        if s == 2 and in_two(j - 1) and (j - 1) // H + 1 < NQ:
                            load_mask(b2, (j - 1) // H + 1, (j - 1) % H)
                        if s in (4, 8) and in_one(i + 1):
                            load_adj(b1, i + 1, s // 8)
                        if s == 6 and in_two(j - 3) and (j - 3) % H == H - 1:
                            store_out(b2, (j - 3) // H)
                        if s == 7 and in_one(i - 3):
                            store_x1(b1, i - 3)
                        if s == 9 and in_two(j - 1) and (j - 1) % H == 0:
                            load_projected(b2, (j - 1) // H)
                        if s == 11 and in_one(i):
                            store_mask(b1, i)
                        if s == 12 and in_one(i + 1):
                            load_hx(b1, i + 1)
                if b1 is not None:
                    for stored in mT_out + hp_out + e_out:
                        sp.wait_ge(stored, NT // 2 * 16)
                    for stored in x1_out:
                        sp.wait_ge(stored, NT // 4 * 16)
                if first:
                    for stored in x0_out:
                        sp.wait_ge(stored, (B - 1) * NQ // 2 * 16)
                if b2 is not None:
                    for stored in out_st:
                        sp.wait_ge(stored, NQ // 2 * 16)

            @block.gpsimd
            def _(pool):
                def whole_values(t):
                    pool.wait_ge(hpl_in[t // 2 % 2], (t // 4 + 1) * 16)
                    pool.wait_ge(exp_ok, 2)
                    free(pool, val_ok, t - 2)
                    vt, hv = vf[t % 3], hpl[t // 2 % 2][:, t % 2, :].rearrange("p (h e) -> p h e", h=H)
                    for i, e in enumerate((eB, eB1)):
                        ee = e[:, t, :]
                        nc.gpsimd.tensor_tensor(vt[:, :, i * (E + 1):i * (E + 1) + E], hv, over(ee, 2, [P, H, E]), ALU.mult)
                        ins = nc.gpsimd.tensor_copy(vt[:, :, i * (E + 1) + E], ee)
                    ins.then_inc(whole_ok, 1)

                if b2 is not None:
                    for t in range(NT):
                        whole_values(t)
                if b1 is None:
                    return
                for k in range(NT):
                    pool.wait_ge(idx_ok, k + 1)
                    for g in range(NR):
                        free(pool, red_ok, 2 * ((k - 1) * NR + g + 1) if k else 0)
                        for i, s in enumerate(GROUPS[g]):
                            pool.indirect_dma_start(
                                out=gath[g][:, i, :], out_offset=None, in_=table[0:ROWS] if first else table,
                                in_offset=bass.IndirectOffsetOnAxis(ap=idx[k % 2][:, s:s + 1], axis=0),
                            ).then_inc(g_in[s], 16)
                for s in range(S):
                    pool.wait_ge(g_in[s], NT * 16)

            @block.vector
            def _(dve):
                v = nc.vector
                link = Chain(dve, dve_c, fresh=True).link
                top, rows, norm, quarter = (Chain(dve, dve_c) for _ in range(4))

                def first_neighbours(k, piece):
                    top.ready()
                    if piece == 0:
                        dve.wait_ge(keys_ok, k + 1)
                        top.done(v.scalar_tensor_tensor(key[:], kps[:, 0:NG], 0.0, base[:], ALU.is_gt, ALU.mult))
                    elif piece == 1:
                        v.tensor_tensor(key[:], key[:], kps[:, 0:NG], ALU.add).then_inc(bytes_ok, 1)
                        dve.wait_ge(bytes_ok, k + 1)
                    elif piece < 9:
                        r, replace = divmod(piece - 2, 2)
                        eight = k32[:, 8 * r:8 * r + 8]
                        if replace:
                            top.done(v.match_replace(out=key[:], in_to_replace=eight, in_values=key[:], imm_value=0.0))
                        else:
                            top.done(v.max(eight, key[:]))
                    elif piece == 9:
                        top.done(v.tensor_copy(ki[:], k32[:, 0:S]))
                    elif piece == 10:
                        v.tensor_scalar(b8[:], ki[:], 8, 3, ALU.logical_shift_right, ALU.logical_shift_left)
                        top.done(v.tensor_tensor(an[:], over(ki[:], 2, [P, S, GB]), over(bitc[:], 1, [P, S, GB]),
                                                 ALU.bitwise_and))
                    elif piece == 11:
                        top.done(v.tensor_tensor(cand[:].rearrange("p (s g) -> p s g", s=S), over(b8[:], 2, [P, S, GB]),
                                                 over(ofsc[:], 1, [P, S, GB]), ALU.subtract))
                    elif piece == 12:
                        top.done(v.scalar_tensor_tensor(cand[:], an[:].rearrange("p s g -> p (s g)"), 0.0,
                                                        cand[:], ALU.is_gt, ALU.mult))
                    elif piece < 20:
                        r, replace = divmod(piece - 13, 2)
                        eight = c32[:, 8 * r:8 * r + 8]
                        if replace:
                            top.done(v.match_replace(out=cand[:], in_to_replace=eight, in_values=cand[:], imm_value=0.0))
                        else:
                            top.done(v.max(eight, cand[:]))
                    else:
                        v.tensor_scalar(idx[k % 2][:], c32[:, 0:S], -1.0, rowbase[:, 0:1], ALU.mult, ALU.add)\
                         .then_inc(idx_ok, 1)
                        if k == 0:
                            top.done(v.tensor_copy(degmin[:], c32[:, 0:1]))
                        else:
                            top.done(v.tensor_tensor(degmin[:], degmin[:], c32[:, 0:1], ALU.min))

                def take_max(k, g, half):
                    if half == 0:
                        for s in GROUPS[g]:
                            dve.wait_ge(g_in[s], (k + 1) * 16)
                    c = slice(half * P, (half + 1) * P)
                    v.tensor_reduce(part[:, g, c], gath[g][:, :, c].rearrange("p s c -> p c s"), AX_X, ALU.max)\
                     .then_inc(red_ok, 1)

                def whole_max(k):
                    dve.wait_ge(red_ok, (k + 1) * 2 * NR)
                    v.tensor_tensor(agg[:], part[:, 0, :], part[:, 1, :], ALU.max).then_inc(agg_ok, 1)

                def residual_norm(k, piece):
                    if piece == 0:
                        dve.wait_ge(lin_ok, k + 1)
                        wait_hx(dve, k)
                        v.scalar_tensor_tensor(x1[k % 4], kps[:, NG:2 * NG], 0.0, hx[k % 4][:, 1, :],
                                               ALU.max, ALU.add).then_inc(x1_ok, 1)
                    elif piece == 1:
                        dve.wait_ge(x1_ok, k + 1)
                        norm.done(v.bn_stats(st1[:], x1[k % 4]))
                    elif piece == 2:
                        norm.ready()
                        v.bn_aggr(mv1[:], st1[:]).then_inc(var1_ok, 1)
                    elif piece == 3:
                        dve.wait_ge(root1_ok, k + 1)
                        norm.done(v.reciprocal(rs1[:, 0:1], rs1[:, 0:1]))
                    else:
                        norm.ready()
                        v.scalar_tensor_tensor(rs1[:, 1:2], mv1[:, 0:1], -1.0, rs1[:, 0:1], ALU.mult, ALU.mult)\
                         .then_inc(ln1_ok, 1)

                def norm_quarter(c, piece):
                    r = rs0[c % 2]
                    quarter.ready()
                    if piece == 0:
                        dve.wait_ge(x0_in[c % 2], (c // 2 + 1) * 16)
                        for t in range(Q):
                            ins = v.bn_stats(st0[:, t, :], x0[c % 2][:, t, :])
                        quarter.done(ins)
                    elif piece == 1:
                        for t in range(Q):
                            ins = v.bn_aggr(mv0[:, t, :], st0[:, t, :])
                        quarter.done(ins)
                    elif piece == 2:
                        v.tensor_copy(r[:], mv0[:, :, 1]).then_inc(x0_var, 1)
                    elif piece == 3:
                        dve.wait_ge(x0_root, c + 1)
                        quarter.done(v.reciprocal(r[:], r[:]))
                    else:
                        v.scalar_tensor_tensor(nm0[c % 2][:], mv0[:, :, 0], -1.0, r[:], ALU.mult, ALU.mult)\
                         .then_inc(x0_norm, 1)

                def factors():
                    link(v.tensor_copy(sd2[:], sd[:]))
                    dve.sem_inc(sd_ok, 1)
                    s2, d2 = sd2[:, :, 0:H], sd2[:, :, H:2 * H]
                    v.tensor_scalar(kd[:], d2, BIG, None, ALU.mult)
                    link(v.tensor_scalar(negd[:], d2, -1.0, None, ALU.mult))
                    v.tensor_reduce(dmm[:, 0:H], d2.rearrange("p t h -> p h t"), AX_X, ALU.max)
                    v.tensor_reduce(dmm[:, H:2 * H], negd[:].rearrange("p t h -> p h t"), AX_X, ALU.max).then_inc(dd_ok, 1)
                    dve.wait_ge(dT_ps, 1)
                    link(v.tensor_reduce(drow[:], cps[0:2 * H, 0:P], AX_X, ALU.max))
                    v.tensor_scalar(ddiag[:], ident[0:2 * H, 0:2 * H], drow[:, 0:1], None, ALU.mult).then_inc(dd_ok, 1)
                    dve.wait_ge(db_ps, 1)
                    link(v.tensor_copy(dmax[:], cps[:, P:P + 2 * H]))
                    dmx = over(dmax[:, 0:H], 1, [P, NT, H])
                    v.tensor_tensor(tmpz[:], d2, dmx, ALU.subtract).then_inc(exp_in, 1)
                    link(v.tensor_tensor(tmpn[:], s2, dmx, ALU.add))
                    link(v.tensor_scalar(tmpp[:], tmpn[:], 0.0, None, ALU.max))
                    v.tensor_scalar(tmpn[:], tmpn[:], 0.0, None, ALU.min).then_inc(exp_in, 1)
                    link(v.tensor_reduce(gtmp[:, 0:1], dmax[:], AX_X, ALU.max))
                    link(v.tensor_scalar(gtmp[:, 0:1], gtmp[:, 0:1], 1.0e18, None, ALU.is_le))
                    link(v.tensor_tensor(good[:, 0:1], good[:, 0:1], gtmp[:, 0:1], ALU.min))
                    link(v.tensor_tensor(gtmp[:], dmax[:, 0:H], dmax[:, H:2 * H], ALU.add))
                    link(v.tensor_scalar(gtmp[:], gtmp[:], RANGE, None, ALU.is_le))
                    link(v.tensor_reduce(gtmp[:, 0:1], gtmp[:], AX_X, ALU.min))
                    link(v.tensor_tensor(good[:, 2:3], good[:, 2:3], gtmp[:, 0:1], ALU.min))
                    dve.wait_ge(exp_ok, 4)

                def values(t, piece):
                    vt, o = vf[t % 3], val[:, t * H:(t + 1) * H]
                    if piece == 1:
                        dve.wait_ge(first_ok, t + 1)
                        v.tensor_tensor(vt, vt, o[:, :, 0, :], ALU.subtract).then_inc(rest_ok, 1)
                    else:
                        dve.wait_ge(second_ok, t + 1)
                        v.tensor_tensor(o[:, :, 2, :], vt, o[:, :, 1, :], ALU.subtract).then_inc(val_ok, 1)

                def unit_edges(n):
                    u, jt = divmod(n, NT)
                    q = u // H
                    if jt == 0:
                        dve.wait_ge(maskq_in[q % 2], (q // 2 + 1) * 16 * Q)
                    dve.wait_ge(relu_ok, n + 1)
                    free(dve, gt_used, n + 1 - D)
                    v.tensor_tensor(gt[n % D][:].rearrange("p (t r) -> p t r", t=Q),
                                    rb[n % D][:].rearrange("p (t r) -> p t r", t=Q),
                                    maskq[q % 2][:, :, jt, :], ALU.min).then_inc(gt_ok, 1)

                def each(ap, n=E):
                    return over(ap, 2, [P, Q, n])

                def unit_rows(u, piece):
                    q, h = u // H, u % H
                    t4 = slice(q * Q, (q + 1) * Q)
                    rows.ready()
                    if piece == 0:
                        dve.wait_ge(araw_ok, (u + 1) * Q)
                        rows.done(v.tensor_tensor(gs, gs, araw[:, :, 1, :], ALU.add))
                    elif piece == 1:
                        rows.done(v.tensor_tensor(gs, gs, araw[:, :, 2, :], ALU.add))
                    elif piece == 2:
                        dve.wait_ge(mraw_ok, 2 * (u + 1))
                        rows.done(v.tensor_tensor(ms, ms, mraw[:, :, 1, :], ALU.add))
                    elif piece == 3:
                        rows.done(v.tensor_tensor(ms, ms, mraw[:, :, 2, :], ALU.add))
                    elif piece == 4:
                        v.tensor_tensor(f0[:], ms, gs[:, :, E + 1:V], ALU.subtract).then_inc(mraw_used, 1)
                        rows.done(v.tensor_tensor(gs[:, :, 0:E + 1], gs[:, :, 0:E + 1], each(eA[:, t4, h], E + 1), ALU.mult))
                    elif piece == 5:
                        rows.done(v.tensor_tensor(f0[:], f0[:], each(eA1[:, t4, h], E + 1), ALU.mult))
                    elif piece == 6:
                        v.tensor_tensor(f0[:], f0[:], gs[:, :, 0:E + 1], ALU.add).then_inc(araw_used, 1)
                        dve.wait_ge(araw_used, u + 1)
                    elif piece == 7:
                        rows.done(v.tensor_scalar(rden[:], f0[:, :, E], 1.0e-37, None, ALU.max))
                    elif piece == 8:
                        rows.done(v.reciprocal(rden[:], rden[:]))
                    elif piece == 9:
                        rows.done(v.tensor_tensor(f1[:], f0[:, :, 0:E], each(rden[:]), ALU.mult))
                    elif piece == 10:
                        rows.done(v.tensor_tensor(f1[:], f1[:], over(bias_b[:, h, :], 1, [P, Q, E]), ALU.add))
                    elif piece == 11:
                        dve.wait_ge(hq_in, (q + 1) * 16)
                        v.scalar_tensor_tensor(f1[:], f1[:], 0.0, hq[:, :, h * E:(h + 1) * E], ALU.max, ALU.add)\
                         .then_inc(hq_used, 1)
                    elif piece == 12:
                        if last:
                            dve.wait_ge(hq_used, u + 1)
                            link(v.tensor_reduce(msum[:], f1[:], AX_X, ALU.add))
                        else:
                            dve.wait_ge(msum_ok, (u + 1) * Q)
                        v.tensor_scalar(negm[:], msum[:], -1.0 / E, None, ALU.mult).then_inc(negm_ok, 1)
                    elif piece == 13:
                        dve.wait_ge(root2_ok, u + 1)
                        rows.done(v.reciprocal(var[:], var[:]))
                    elif piece == 14:
                        v.tensor_tensor(nm2[:], negm[:], var[:], ALU.mult).then_inc(nm2_ok, 1)
                    elif piece == 15:
                        if last:
                            dve.wait_ge(nm2_ok, u + 1)
                            link(v.tensor_tensor(f1[:], f1[:], each(var[:]), ALU.mult))
                            link(v.tensor_tensor(f1[:], f1[:], each(nm2[:]), ALU.add))
                        else:
                            dve.wait_ge(app_ok, (u + 1) * Q)
                        rows.done(v.tensor_tensor(f1[:], f1[:], over(gamma_b[:, h, :], 1, [P, Q, E]), ALU.mult))
                    elif piece == 16:
                        rows.done(v.tensor_tensor(f1[:], f1[:], over(beta_b[:, h, :], 1, [P, Q, E]), ALU.add))
                    else:
                        dve.wait_ge(xq_in, (q + 1) * 16)
                        o = outq[q % 2][:, :, h * E:(h + 1) * E]
                        v.tensor_tensor(o, f1[:], o, ALU.add).then_inc(unit_done, 1)

                TOP = {s: (2 * s, 2 * s + 1) for s in range(0, 10)} | {10: (20, None)}
                ROWS_AT = {4: (0, 1), 5: (2, 3), 6: (4, 5), 7: (6, 7), 8: (8, 9), 9: (10, 11), 12: (12, None)}
                LATE = {0: 13, 1: 14, 4: 15, 5: 16, 6: 17}
                NORM = {7: (0,), 8: (1,), 9: (2,), 11: (3,), 12: (4,)}
                MAXES = {5: (0, 0), 6: (0, 1), 13: (1, 0), 14: (1, 1)}
                for j in STEPS:
                    i = j + 1
                    if j == -1 and b2 is not None:
                        factors()
                    for s in range(NT):
                        for piece in range(5):
                            c = table_quarter(j, s, 2 + piece) if first else None
                            if c is not None:
                                norm_quarter(c, piece)
                        ta, tb = TOP.get(s, (None, None))
                        ra, rb_ = ROWS_AT.get(s, (None, None))
                        if in_two(j - 1):
                            unit_edges((j - 1) * NT + s)
                        if in_one(i - 1) and ta is not None:
                            first_neighbours(i - 1, ta)
                        if in_two(j - 2) and ra is not None:
                            unit_rows(j - 2, ra)
                        if in_two(j - 3) and s in LATE:
                            unit_rows(j - 3, LATE[s])
                        for piece in NORM.get(s, ()):
                            if in_one(i - 3):
                                residual_norm(i - 3, piece)
                        if in_one(i - 1) and tb is not None:
                            first_neighbours(i - 1, tb)
                        if in_two(j - 2) and rb_ is not None:
                            unit_rows(j - 2, rb_)
                        if in_one(i - 2) and s in MAXES:
                            take_max(i - 2, *MAXES[s])
                        if in_one(i - 2) and s == 15:
                            whole_max(i - 2)
                        for piece in (1, 2):
                            if b2 is not None and 0 <= j * NT + s - piece < NT:
                                values(j * NT + s - piece, piece)
                    if i == NT and b1 is not None:
                        top.ready()
                        link(v.tensor_scalar(rowbase[:], rowbase[:], float(ROWS), None, ALU.add))
                        link(v.tensor_scalar(degmin[:], degmin[:], 0.0, None, ALU.is_gt))
                        link(v.tensor_tensor(good[:, 1:2], good[:, 1:2], degmin[:], ALU.min))
                        dve.wait_ge(mT_ok, 2 * NT)
                        link(v.tensor_reduce(gtmp[:, 0:2], chk[:], AX_X, ALU.add))
                        link(v.tensor_scalar(gtmp[:, 0:1], gtmp[:, 0:1], -float(NT * N), None, ALU.add))
                        link(v.scalar_tensor_tensor(gtmp[:, 0:1], gtmp[:, 1:2], -8.0, gtmp[:, 0:1], ALU.mult, ALU.add))
                        link(v.tensor_tensor(odd[:], odd[:], gtmp[:, 0:1], ALU.add))
            @block.tensor
            def _(pe):
                mm, turn = nc.tensor.matmul, nc.tensor.transpose

                def turn_activations(k):
                    pe.wait_ge(agg_ok, k + 1)
                    if k == 0 and both:
                        pe.wait_ge(exp_in, 1)
                    wait_hx(pe, k)
                    free(pe, hp_ok, 3 * k)
                    for i in range(2):
                        turn(cps[:, i * P:(i + 1) * P], hx[k % 4][:, 0, i * P:(i + 1) * P], ident[:])
                    for i in range(2):
                        ins = turn(cps[:, (2 + i) * P:(3 + i) * P], agg[:, i * P:(i + 1) * P], ident[:])
                    ins.then_inc(hT_ps, 1)

                def turn_mask(k, hf):
                    m = 2 * k + hf
                    pe.wait_ge(mask_ok, m + 1)
                    free(pe, mT_ok, m)
                    for i in range(NT // 2):
                        ins = turn(tps[:, i * P:(i + 1) * P], mask_h[hf][:, i * P:(i + 1) * P], identb[:])
                    ins.then_inc(turn_ok, 1)

                def dense0(k):
                    pe.wait_ge(hT_ok, k + 1)
                    free(pe, x1_ok, k)
                    free(pe, bytes_ok, min(k + 3, NT))
                    o = kps[:, NG:2 * NG]
                    for i in range(4):
                        mm(o, hT[:, i, :], w0_sb[:, i, :], start=(i == 0), stop=False)
                    mm(o, ones[0:1, :], b0_sb[:], start=False, stop=True).then_inc(lin_ok, 1)

                def group_bytes(k):
                    pe.wait_ge(mT_ok, 2 * k + 2)
                    free(pe, x1_ok, k - 2)
                    free(pe, bytes_ok, k)
                    for t in range(NT):
                        ins = mm(kps[:, t * GPT:(t + 1) * GPT], mT[k % 2][:, t, :], bits_w[:], start=True, stop=True)
                    ins.then_inc(keys_ok, 1)

                def turn_h1(k):
                    pe.wait_ge(h1_ok, k + 1)
                    for i in range(2):
                        ins = turn(cps[:, i * P:(i + 1) * P], h1[:, i * P:(i + 1) * P], ident[:])
                    ins.then_inc(h1T_ps, 1)

                def project1(k):
                    pe.wait_ge(h1T_ok, k + 1)
                    for i in range(2):
                        mm(cps[:, 0:W1N], h1T[:, i, :], r1[:, i, :], start=(i == 0), stop=(i == 1))
                    for i in range(2):
                        ins = mm(cps[0:H, 3 * P:4 * P], r1[:, i, C:C + H], h1T[:, i, :], start=(i == 0), stop=(i == 1))
                    ins.then_inc(hp_ps, 1)

                def factors():
                    pe.wait_ge(dd_ok, 1)
                    turn(cps[0:2 * H, 0:P], dmm[:], ident[:]).then_inc(dT_ps, 1)
                    pe.wait_ge(dd_ok, 2)
                    mm(cps[:, P:P + 2 * H], ones[0:2 * H, :], ddiag[:], start=True, stop=True).then_inc(db_ps, 1)

                def unit_edges(n):
                    u, jt = divmod(n, NT)
                    h = u % H
                    pe.wait_ge(gt_ok, n + 1)
                    for t in range(Q):
                        if jt == 0:
                            free(pe, araw_ok, (u - 1) * Q + t + 1)
                        ins = mm(acc[t][:, 0:K3 * V], gt[n % D][:, t * P:(t + 1) * P],
                                 val[:, jt * H + h].rearrange("p k v -> p (k v)"), start=(jt == 0), stop=(jt == NT - 1))
                    ins.then_inc(gt_used, 1)

                def unit_masked(u, pair, part_of):
                    q, h, w = u // H, u % H, K3 * (E + 1)
                    if part_of == 0:
                        pe.wait_ge(maskq_in[q % 2], (q // 2 + 1) * 16 * Q)
                        if u == 0 and pair == 0:
                            pe.wait_ge(val_ok, NT)
                        free(pe, mraw_ok, 2 * u + pair)
                    i = part_of // 2
                    for jt in range(part_of % 2 * (NT // 2), (part_of % 2 + 1) * (NT // 2)):
                        ins = mm(macc[:, i * w:(i + 1) * w], maskq[q % 2][:, 2 * pair + i, jt, :],
                                 val[:, jt * H + h, :, E + 1:V], start=(jt == 0), stop=(jt == NT - 1))
                    if part_of == 3:
                        ins.then_inc(macc_ok, 1)

                for j in STEPS:
                    i = j + 1
                    if j == -1 and b2 is not None:
                        factors()
                    for s in range(NT):
                        if s == 1 and in_one(i - 3):
                            turn_activations(i - 3)
                        if s == 5 and in_one(i):
                            turn_mask(i, 0)
                        if s == 5 and in_one(i - 3):
                            dense0(i - 3)
                        if s == 9 and in_one(i):
                            turn_mask(i, 1)
                        if s == 13 and in_one(i):
                            group_bytes(i)
                        if s == 13 and in_one(i - 3):
                            turn_h1(i - 3)
                        if s == 15 and in_one(i - 3):
                            project1(i - 3)
                        if in_two(j - 1) and 2 <= s < 6:
                            unit_masked(j - 1, 0, s - 2)
                        if in_two(j - 1) and 9 <= s < 13:
                            unit_masked(j - 1, 1, s - 9)
                        n = (j - 1) * NT + s - BEHIND
                        if b2 is not None and 0 <= n < NQ * H * NT:
                            unit_edges(n)

            @block.scalar
            def _(act):
                a = nc.scalar

                def activations_out(k):
                    act.wait_ge(hT_ps, k + 1)
                    a.copy(hT[:].rearrange("p i r -> p (i r)"), cps[:]).then_inc(hT_ok, 1)

                def make_mask(k, hf):
                    m = 2 * k + hf
                    act.wait_ge(adj_in[hf], (k + 1) * 16)
                    free(act, turn_ok, m - 1)
                    a.activation(mask_h[hf][:], adj_h[hf][:], ACT.Square, bias=minus1[:, 0:1], scale=4.0,
                                 accum_out=chk[:, 0, m:m + 1]).then_inc(mask_ok, 1)

                def mask_out(k, hf):
                    m = 2 * k + hf
                    act.wait_ge(turn_ok, m + 1)
                    if hf == 0:
                        free(act, mT_out[k % 2], k // 2 * 16)
                    a.activation(mT[k % 2][:, hf * (NT // 2):(hf + 1) * (NT // 2), :].rearrange("p t r -> p (t r)"), tps[:],
                                 ACT.Sign, bias=minus1[:, 0:1], accum_out=chk[:, 1, m:m + 1])\
                     .then_inc(mT_ok, 1)

                def root1(k):
                    act.wait_ge(var1_ok, k + 1)
                    a.activation(rs1[:, 0:1], mv1[:, 1:2], ACT.Sqrt, bias=epsc[:, 0:1]).then_inc(root1_ok, 1)

                def normalise(k):
                    act.wait_ge(ln1_ok, k + 1)
                    a.activation(h1[:], x1[k % 4], ACT.Relu, bias=rs1[:, 1:2], scale=rs1[:, 0:1]).then_inc(h1_ok, 1)

                def h1_out(k):
                    act.wait_ge(h1T_ps, k + 1)
                    a.copy(h1T[:].rearrange("p i r -> p (i r)"), cps[:, 0:2 * P]).then_inc(h1T_ok, 1)

                def projected_out(k):
                    act.wait_ge(hp_ps, k + 1)
                    free(act, hp_out[k % 2], k // 2 * 16)
                    free(act, e_out[k % 2], k // 2 * 16)
                    if k == 0 and both:
                        act.wait_ge(sd_ok, 1)
                    a.copy(hps[k % 2][:], cps[:, 0:C]).then_inc(hp_ok, 1)
                    a.copy(sd[:, k, :], cps[:, C:W1N]).then_inc(hp_ok, 1)
                    a.copy(eT[k % 2][:], cps[0:H, 3 * P:4 * P]).then_inc(hp_ok, 1)

                def table_root(c):
                    act.wait_ge(x0_var, c + 1)
                    a.activation(rs0[c % 2][:], rs0[c % 2][:], ACT.Sqrt, bias=epsc[:, 0:1]).then_inc(x0_root, 1)

                def table_rows(c):
                    act.wait_ge(x0_norm, c + 1)
                    for t in range(Q):
                        a.activation(x0[c % 2][:, t, :], x0[c % 2][:, t, :], ACT.Relu, bias=nm0[c % 2][:, t:t + 1],
                                     scale=rs0[c % 2][:, t:t + 1]).then_inc(x0_relu, 1)

                def factors():
                    act.wait_ge(exp_in, 1)
                    a.activation(eB[:], tmpz[:], ACT.Exp).then_inc(exp_ok, 1)
                    a.activation(eB1[:], tmpz[:], ACT.Exp, scale=SLOPE).then_inc(exp_ok, 1)
                    act.wait_ge(exp_in, 2)
                    a.activation(eA[:], tmpn[:], ACT.Exp, scale=1.0 - SLOPE).then_inc(exp_ok, 1)
                    a.activation(eA1[:], tmpp[:], ACT.Exp, scale=SLOPE - 1.0).then_inc(exp_ok, 1)

                def values(t, part_of):
                    act.wait_ge(rest_ok if part_of else whole_ok, t + 1)
                    a.copy(val[:, t * H:(t + 1) * H, part_of, :], vf[t % 3]).then_inc(second_ok if part_of else first_ok, 1)

                def sums_out(u):
                    act.wait_ge(gt_used, (u + 1) * NT)
                    free(act, araw_used, u)
                    for t in range(Q):
                        a.copy(araw[:, t].rearrange("p k v -> p (k v)"), acc[t][:, 0:K3 * V]).then_inc(araw_ok, 1)

                def masked_out(u, pair):
                    act.wait_ge(macc_ok, 2 * u + pair + 1)
                    free(act, mraw_used, u)
                    a.copy(mraw[:, 2 * pair:2 * pair + 2].rearrange("p t k v -> p (t k v)"), macc[:, 0:2 * K3 * (E + 1)])\
                     .then_inc(mraw_ok, 1)

                def unit_signs(n):
                    u, jt = divmod(n, NT)
                    h = u % H
                    if jt == 0:
                        act.wait_ge(srcb_in[h % 2], (u // 2 + 1) * 16)
                    free(act, gt_ok, n + 1 - D)
                    a.activation(rb[n % D][:], srcb[h % 2][:], ACT.Relu, bias=kd[:, jt, h:h + 1], scale=BIG).then_inc(relu_ok, 1)

                def row_sums(u):
                    act.wait_ge(hq_used, u + 1)
                    for t in range(Q):
                        a.activation(f0[:, t, 0:E], f1[:, t, :], ACT.Identity, accum_out=msum[:, t:t + 1]).then_inc(msum_ok, 1)

                def row_squares(u):
                    act.wait_ge(negm_ok, u + 1)
                    for t in range(Q):
                        a.activation(f0[:, t, 0:E], f1[:, t, :], ACT.Square, bias=negm[:, t:t + 1],
                                     accum_out=var[:, t:t + 1]).then_inc(sq2_ok, 1)
                    act.wait_ge(sq2_ok, (u + 1) * Q)
                    a.activation(var[:], var[:], ACT.Sqrt, bias=epsc[:, 1:2], scale=1.0 / E).then_inc(root2_ok, 1)

                def row_scale(u):
                    act.wait_ge(nm2_ok, u + 1)
                    for t in range(Q):
                        a.activation(f1[:, t, :], f1[:, t, :], ACT.Identity, bias=nm2[:, t:t + 1],
                                     scale=var[:, t:t + 1]).then_inc(app_ok, 1)

                for j in STEPS:
                    i = j + 1
                    if j == -1 and b2 is not None:
                        factors()
                    for s in range(NT):
                        n = (j - 1) * NT + s + AHEAD
                        if b2 is not None and 0 <= n < NQ * H * NT:
                            unit_signs(n)
                        if first:
                            for offset, piece in ((4, table_root), (7, table_rows)):
                                c = table_quarter(j, s, offset)
                                if c is not None:
                                    piece(c)
                        for part_of in range(2):
                            if b2 is not None and 0 <= j * NT + s - part_of < NT:
                                values(j * NT + s - part_of, part_of)
                        if s == 0 and in_one(i - 4):
                            projected_out(i - 4)
                        if s == 2 and in_two(j - 2):
                            sums_out(j - 2)
                        if s in (3, 7) and in_one(i):
                            make_mask(i, s // 7)
                        if s == 3 and in_one(i - 3):
                            activations_out(i - 3)
                        if s == 6 and in_two(j - 1):
                            masked_out(j - 1, 0)
                        if s in (6, 10) and in_one(i):
                            mask_out(i, s // 8)
                        if s == 10 and in_one(i - 3):
                            root1(i - 3)
                        if s == 10 and in_two(j - 2) and not last:
                            row_sums(j - 2)
                        if s == 13 and in_two(j - 2):
                            row_squares(j - 2)
                        if s == 12 and in_one(i - 3):
                            normalise(i - 3)
                        if s == 14 and in_one(i - 3):
                            h1_out(i - 3)
                        if s == 14 and in_two(j - 1):
                            masked_out(j - 1, 1)
                        if s == 2 and in_two(j - 3) and not last:
                            row_scale(j - 3)

        def direct_attention():
            adjg = sb("adjg", [P, N], I32)
            wgt = sb("wgt", [P, N])
            term = sb("term", [P, N])
            dstb = [sb(f"dstb{i}", [P, N]) for i in range(2)]
            hpg = sb("hpg", [P, NT, C])
            a_all = [sb(f"a_all{i}", [P, H, T, E]) for i in range(2)]
            prod = sb("prod", [P, H, T, E])
            sg = sb("sg", [P, NT, 2, H * T])
            dT = sb("dT", [H * T, N])
            pT = sb("pT", [P, N])
            sk = sb("sk", [P, H * T])
            hpk, xk, one = sb("hpk", [P, C]), sb("xk", [P, C]), sb("one", [P, E])
            mx, den, st, mv, root = (sb("mx", [P, 1]), sb("den", [P, 1]), sb("st", [P, 6]), sb("mv", [P, 2]),
                                     sb("root", [P, 1]))
            src_all = scratch("src_all", (NT, P, H * T))
            dst_all = scratch("dst_all", (H * T, N))
            gps = [ps(f"gps{i}", [P, 512]) for i in range(4)]
            ops = ps("ops", [P, 512])

            with nc.Fori(0, B) as b:
                with nc.Block() as block:
                    @block.sync
                    def _(sp):
                        sp.dma_start(hpg[:], hp_d[b].rearrange("t p c -> p t c")).then_inc(gen_in, 16)
                        for dst, a in zip(a_all, (a_src, a_dst)):
                            sp.dma_start(dst[:], a.partition_broadcast(P)).then_inc(gen_in, 16)
                        sp.wait_ge(sg_ok, NT)
                        sp.dma_start(src_all.rearrange("t p c -> p t c"), sg[:, :, 0, :]).then_inc(gen_out, 16)
                        sp.wait_ge(dT_ok, 4)
                        sp.dma_start(dst_all, dT[:]).then_inc(gen_out, 16)
                        sp.wait_ge(gen_out, 32)

                    @block.vector
                    def _(dve):
                        link = Chain(dve, dve_c, fresh=True).link
                        dve.wait_ge(gen_in, 48)
                        for t in range(NT):
                            for i in range(2):
                                hv = hpg[:, t, :].rearrange("p (h e) -> p h e", h=H)
                                for y in range(T):
                                    ins = nc.vector.tensor_tensor(prod[:, :, y, :], hv, a_all[i][:, :, y, :], ALU.mult)
                                link(ins)
                                link(nc.vector.tensor_reduce(sg[:, t, i, :], prod[:].rearrange("p h y e -> p (h y) e"),
                                                             AX_X, ALU.add))
                            dve.sem_inc(sg_ok, 1)

                    @block.tensor
                    def _(pe):
                        for t in range(NT):
                            pe.wait_ge(sg_ok, t + 1)
                            nc.tensor.transpose(gps[t // 4][0:H * T, t % 4 * P:(t % 4 + 1) * P], sg[:, t, 1, :], ident[:])\
                              .then_inc(dT_t, 1)

                    @block.scalar
                    def _(act):
                        for g in range(4):
                            act.wait_ge(dT_t, 4 * (g + 1))
                            nc.scalar.copy(dT[:, g * 4 * P:(g + 1) * 4 * P], gps[g][0:H * T, :]).then_inc(dT_ok, 1)
                reset()

                with nc.Fori(0, NT) as k:
                    with nc.Block() as block:
                        @block.sync
                        def _(sp):
                            for dst, src in ((adjg[:], adj.rearrange("b (k p) j -> b k p j", p=P)[b, k]),
                                             (sk[:], src_all[k]), (hpk[:], hp_d[b, k]), (xk[:], x1_d[b, k])):
                                sp.dma_start(dst, src).then_inc(row_in, 16)
                            for n in range(H * T):
                                free(sp, dst_used, n - 1)
                                sp.dma_start(dstb[n % 2][:], dst_all[n].partition_broadcast(P)).then_inc(dst_in[n % 2], 16)
                            sp.wait_ge(head_ok, H)
                            sp.dma_start(out.rearrange("b (k p) c -> b k p c", p=P)[b, k], xk[:]).then_inc(gen_out, 16)
                            sp.wait_ge(gen_out, 16)

                        @block.vector
                        def _(dve):
                            v = nc.vector
                            link = Chain(dve, dve_c, fresh=True).link
                            dve.wait_ge(row_in, 64)
                            for h in range(H):
                                free(dve, pT_ps, 4 * h)
                                for t in range(T):
                                    n = h * T + t
                                    dve.wait_ge(dst_in[n % 2], (n // 2 + 1) * 16)
                                    v.tensor_scalar(term[:], dstb[n % 2][:], sk[:, n:n + 1], None, ALU.add).then_inc(dst_used, 1)
                                    dve.wait_ge(dst_used, n + 1)
                                    link(v.scalar_tensor_tensor(term[:] if t else wgt[:], adjg[:], float(t + 1), term[:],
                                                                ALU.is_equal, ALU.mult))
                                    if t:
                                        link(v.tensor_tensor(wgt[:], wgt[:], term[:], ALU.add))
                                link(v.scalar_tensor_tensor(wgt[:], wgt[:], SLOPE, wgt[:], ALU.mult, ALU.max))
                                link(v.tensor_scalar(term[:], adjg[:], 0.0, NEG, ALU.is_equal, ALU.mult))
                                link(v.tensor_tensor(wgt[:], wgt[:], term[:], ALU.add))
                                link(v.tensor_reduce(mx[:], wgt[:], AX_X, ALU.max))
                                v.tensor_scalar(mx[:], mx[:], -1.0, None, ALU.mult).then_inc(w_ok, 1)
                                dve.wait_ge(p_ok, h + 1)
                                dve.wait_ge(o_ps, h + 1)
                                link(v.reciprocal(den[:], den[:]))
                                link(v.tensor_scalar(one[:], ops[:, 0:E], den[:, 0:1], None, ALU.mult))
                                link(v.tensor_tensor(one[:], one[:], bias_b[:, h, :], ALU.add))
                                link(v.scalar_tensor_tensor(one[:], one[:], 0.0, hpk[:, h * E:(h + 1) * E], ALU.max, ALU.add))
                                link(v.bn_stats(st[:], one[:]))
                                link(v.bn_aggr(mv[:], st[:]))
                                dve.sem_inc(mv_ok, 1)
                                dve.wait_ge(root_ok, h + 1)
                                link(v.reciprocal(root[:], root[:]))
                                link(v.tensor_scalar(one[:], one[:], mv[:, 0:1], root[:, 0:1], ALU.subtract, ALU.mult))
                                link(v.tensor_tensor(one[:], one[:], gamma_b[:, h, :], ALU.mult))
                                link(v.tensor_tensor(one[:], one[:], beta_b[:, h, :], ALU.add))
                                xh = xk[:, h * E:(h + 1) * E]
                                v.tensor_tensor(xh, xh, one[:], ALU.add).then_inc(head_ok, 1)
                                dve.wait_ge(head_ok, h + 1)

                        @block.scalar
                        def _(act):
                            for h in range(H):
                                act.wait_ge(w_ok, h + 1)
                                nc.scalar.activation(wgt[:], wgt[:], ACT.Exp, bias=mx[:, 0:1], accum_out=den[:, 0:1])\
                                  .then_inc(p_ok, 1)
                                for g in range(4):
                                    act.wait_ge(pT_ps, 4 * h + g + 1)
                                    free(act, o_ps, h)
                                    nc.scalar.copy(pT[:, g * 4 * P:(g + 1) * 4 * P], gps[g][:]).then_inc(pT_ok, 1)
                                act.wait_ge(mv_ok, h + 1)
                                nc.scalar.activation(root[:], mv[:, 1:2], ACT.Sqrt, bias=epsc[:, 1:2]).then_inc(root_ok, 1)

                        @block.tensor
                        def _(pe):
                            for h in range(H):
                                pe.wait_ge(p_ok, h + 1)
                                for g in range(4):
                                    free(pe, pT_ok, 4 * (h - 1) + g + 1)
                                    for t in range(4 * g, 4 * g + 4):
                                        ins = nc.tensor.transpose(gps[g][:, t % 4 * P:(t % 4 + 1) * P],
                                                                  wgt[:, t * P:(t + 1) * P], ident[:])
                                    ins.then_inc(pT_ps, 1)
                                pe.wait_ge(pT_ok, 4 * (h + 1))
                                for t in range(NT):
                                    ins = nc.tensor.matmul(ops[:, 0:E], pT[:, t * P:(t + 1) * P],
                                                           hpg[:, t, h * E:(h + 1) * E], start=(t == 0), stop=(t == NT - 1))
                                ins.then_inc(o_ps, 1)
                    reset()

        with ExitStack() as turns:
            turn_of_engines(0, None)
        reset()
        with nc.Fori(0, B - 1) as b:
            with ExitStack() as turns:
                turn_of_engines(b + 1, b)
            reset()
        with ExitStack() as turns:
            turn_of_engines(None, B - 1)

        reset()
        with nc.Block() as block:
            @block.tensor
            def _(pe):
                nc.tensor.matmul(cps[0:1, 0:3], ones[:, 0:1], good[:], start=True, stop=True)
                nc.tensor.matmul(cps[0:1, 3:4], ones[:, 0:1], odd[:], start=True, stop=True).then_inc(good_ps, 1)

            @block.vector
            def _(dve):
                link = Chain(dve, dve_c, fresh=True).link
                dve.wait_ge(good_ps, 1)
                nc.vector.tensor_reduce(gsum[:, 0:1], cps[0:1, 0:3], AX_X, ALU.add)
                link(nc.vector.tensor_scalar(gsum[:, 1:2], cps[0:1, 3:4], 0.5, None, ALU.is_le))
                link(nc.vector.tensor_tensor(gsum[:, 0:1], gsum[:, 0:1], gsum[:, 1:2], ALU.add))
                link(nc.vector.tensor_copy(gsum_i[:], gsum[:, 0:1]))
        reset()
        fast.close()
        all_good = nc.values_load(gsum_i[0:1, 0:1], min_val=0, max_val=3 * P + 1)
        with nc.If(all_good < 3 * P + 1):
            direct_attention()
            nc.all_engine_barrier()
        nc.end_all_ifs()


def constants():
    i = np.arange(P)
    bits = np.where(i[:, None] // GB == np.arange(GPT)[None, :], 1 << (i[:, None] % GB), 0)
    g = np.arange(NG)
    b = np.broadcast_to(np.arange(GB), (P, GB))
    return {
        "c_ident": np.eye(P, dtype=np.float32),
        "c_bits": bits.astype(mybir.dt.np(BF16)),
        "c_base": np.broadcast_to((256 * (NG - g)).astype(np.float32), (P, NG)).copy(),
        "c_bit": (1 << b).astype(np.int32),
        "c_ofs": b.astype(np.int32),
    }


_INS = ["x", "adj", "L0_gnn_W", "L0_gnn_b", "L1_gnn_W", "L1_gnn_a_src", "L1_gnn_a_dst", "L1_gnn_bias",
        "L1_gnn_ln_gamma", "L1_gnn_ln_beta"]


def kernel(**inputs):
    import concourse.bacc as bacc
    from concourse.bass_utils import run_bass_kernel_spmd

    nc = bacc.Bacc("TRN2", target_bir_lowering=False, num_devices=1)
    arrays, args = {}, []
    for name, a in [(n, inputs[n]) for n in _INS] + list(constants().items()):
        a = np.ascontiguousarray(a)
        arrays[name] = a
        args.append(nc.dram_tensor(name, a.shape, mybir.dt.from_np(a.dtype), kind="ExternalInput").ap())
    args.append(nc.dram_tensor("out", (B, N, C), F32, kind="ExternalOutput").ap())
    graph_layers(nc, *args)
    r = run_bass_kernel_spmd(nc, [arrays], core_ids=[0])
    return r.results[0]["out"]
```
